# Optimizing a Trainium2 kernel written in Bass

```python
import numpy as np
import jax
import jax.numpy as jnp

def _softmax(x, axis=-1):
    return jax.nn.softmax(x, axis=axis)

def _gelu(x):
    return jax.nn.gelu(x, approximate=True)

def _silu(x):
    return jax.nn.silu(x)

def _sigmoid(x):
    return jax.nn.sigmoid(x)

def _layernorm(x, axis=-1, eps=1e-05):
    m = jnp.mean(x, axis=axis, keepdims=True)
    v = jnp.var(x, axis=axis, keepdims=True)
    return (x - m) / jnp.sqrt(v + eps)

def _scatter_add(tgt, idx, src, axis=0):
    return tgt.at[idx].add(src)

def _segment_sum(src, seg, n):
    return jax.ops.segment_sum(src, seg, n)
kernel_name = 'mk_hybrid_d1_jaxref_r8_9d45ff'

def setup_inputs(seed: int=0):
    np.random.seed(seed)
    _w = jnp.asarray

    def _L0_attn_a_setup():
        import jax, jax.numpy as jnp
        import numpy as np
        B, T, H = (2, 256, 128)
        I, N, R, K = (256, 16, 64, 4)
        EPS = 1e-06
        key = jax.random.key(seed)
        ks = jax.random.split(key, 8)
        s = lambda k, shape, sc=0.02: jax.random.normal(k, shape, dtype=jnp.float32) * sc
        return dict(x=jax.random.normal(ks[0], (B, T, H), dtype=jnp.float32), norm_scale=jnp.ones((H,), jnp.float32), in_w=s(ks[1], (H, 2 * I)), in_b=jnp.zeros((2 * I,), jnp.float32), conv_w=jax.random.normal(ks[2], (K, I), dtype=jnp.float32) / np.float32(np.sqrt(K * I)), conv_b=jnp.zeros((I,), jnp.float32), xproj_w=s(ks[3], (I, R + 2 * N)), dt_w=s(ks[4], (R, I)), dt_b=s(ks[5], (I,), 0.1), A_log=jnp.tile(jnp.log(jnp.arange(1, N + 1, dtype=jnp.float32))[None, :], (I, 1)), D=jnp.ones((I,), jnp.float32), out_w=s(ks[6], (I, H)), out_b=jnp.zeros((H,), jnp.float32))
    _L0_attn_a_in = _L0_attn_a_setup()

    def _L0_attn_b_setup():
        import jax, jax.numpy as jnp
        import numpy as np
        H = 128
        E = 2 * H
        S_DIM = 128
        B, S = (4, 256)
        key = jax.random.key(seed)
        ks = jax.random.split(key, 6)
        inputs = jax.random.normal(ks[0], (B, S, H), dtype=jnp.float32)
        W_uv = jax.random.normal(ks[1], (H, 2 * E + S_DIM), dtype=jnp.float32) * (1.0 / np.sqrt(H))
        b_uv = jnp.zeros((2 * E + S_DIM,), dtype=jnp.float32)
        gamma = jax.random.normal(ks[2], (2, S_DIM), dtype=jnp.float32) * 0.02
        beta = jnp.zeros((2, S_DIM), dtype=jnp.float32)
        W_out = jax.random.normal(ks[3], (E, H), dtype=jnp.float32) * (1.0 / np.sqrt(E))
        b_out = jnp.zeros((H,), dtype=jnp.float32)
        return {'inputs': inputs, 'W_uv': W_uv, 'b_uv': b_uv, 'gamma': gamma, 'beta': beta, 'W_out': W_out, 'b_out': b_out}
    _L0_attn_b_in = _L0_attn_b_setup()

    def _L0_ffn_setup():
        import jax, jax.numpy as jnp
        import numpy as np
        NUM_EXPERTS = 8
        TOP_K = 2
        HIDDEN = 128
        INTER = 352

        def _moe_forward(hidden_states, router_w, w_gate, w_up, w_down):
            B, S, H = hidden_states.shape
            x = hidden_states.reshape(B * S, H)
            logits = x @ router_w
            probs = jax.nn.softmax(logits, axis=-1)
            top_vals, top_idx = jax.lax.top_k(probs, TOP_K)
            weights = top_vals / jnp.sum(top_vals, axis=-1, keepdims=True)
            out = jnp.zeros_like(x)
            for e in range(NUM_EXPERTS):
                w_e = jnp.sum(weights * (top_idx == e), axis=-1)
                gate_o = x @ w_gate[e]
                up_o = x @ w_up[e]
                inter = up_o * jax.nn.silu(gate_o)
                out = out + w_e[:, None] * (inter @ w_down[e])
            return out.reshape(B, S, H)
        key = jax.random.key(seed)
        k1, k2, k3, k4, k5 = jax.random.split(key, 5)
        hs = jax.random.normal(k1, (4, 256, HIDDEN), dtype=jnp.float32)
        s_h = 1.0 / np.sqrt(HIDDEN)
        s_i = 1.0 / np.sqrt(INTER)
        router_w = jax.random.normal(k2, (HIDDEN, NUM_EXPERTS), dtype=jnp.float32) * s_h
        w_gate = jax.random.normal(k3, (NUM_EXPERTS, HIDDEN, INTER), dtype=jnp.float32) * s_h
        w_up = jax.random.normal(k4, (NUM_EXPERTS, HIDDEN, INTER), dtype=jnp.float32) * s_h
        w_down = jax.random.normal(k5, (NUM_EXPERTS, INTER, HIDDEN), dtype=jnp.float32) * s_i
        return {'hidden_states': hs, 'router_w': router_w, 'w_gate': w_gate, 'w_up': w_up, 'w_down': w_down}
    _L0_ffn_in = _L0_ffn_setup()
    _d = {'L0_attn_a_x': _L0_attn_a_in['x'], 'L0_attn_a_norm_scale': _L0_attn_a_in['norm_scale'], 'L0_attn_a_in_w': _L0_attn_a_in['in_w'], 'L0_attn_a_in_b': _L0_attn_a_in['in_b'], 'L0_attn_a_conv_w': _L0_attn_a_in['conv_w'], 'L0_attn_a_conv_b': _L0_attn_a_in['conv_b'], 'L0_attn_a_xproj_w': _L0_attn_a_in['xproj_w'], 'L0_attn_a_dt_w': _L0_attn_a_in['dt_w'], 'L0_attn_a_dt_b': _L0_attn_a_in['dt_b'], 'L0_attn_a_A_log': _L0_attn_a_in['A_log'], 'L0_attn_a_D': _L0_attn_a_in['D'], 'L0_attn_a_out_w': _L0_attn_a_in['out_w'], 'L0_attn_a_out_b': _L0_attn_a_in['out_b'], 'L0_attn_b_W_uv': _L0_attn_b_in['W_uv'], 'L0_attn_b_b_uv': _L0_attn_b_in['b_uv'], 'L0_attn_b_gamma': _L0_attn_b_in['gamma'], 'L0_attn_b_beta': _L0_attn_b_in['beta'], 'L0_attn_b_W_out': _L0_attn_b_in['W_out'], 'L0_attn_b_b_out': _L0_attn_b_in['b_out'], 'L0_ffn_router_w': _L0_ffn_in['router_w'], 'L0_ffn_w_gate': _L0_ffn_in['w_gate'], 'L0_ffn_w_up': _L0_ffn_in['w_up'], 'L0_ffn_w_down': _L0_ffn_in['w_down']}
    _x0 = _d['L0_attn_a_x']
    _d['L0_attn_a_x'] = jax.random.normal(jax.random.fold_in(jax.random.key(seed), 1), (8, 256, 128), dtype=_x0.dtype)
    del _x0
    return _d

def reference(L0_attn_a_x, L0_attn_a_norm_scale, L0_attn_a_in_w, L0_attn_a_in_b, L0_attn_a_conv_w, L0_attn_a_conv_b, L0_attn_a_xproj_w, L0_attn_a_dt_w, L0_attn_a_dt_b, L0_attn_a_A_log, L0_attn_a_D, L0_attn_a_out_w, L0_attn_a_out_b, L0_attn_b_W_uv, L0_attn_b_b_uv, L0_attn_b_gamma, L0_attn_b_beta, L0_attn_b_W_out, L0_attn_b_b_out, L0_ffn_router_w, L0_ffn_w_gate, L0_ffn_w_up, L0_ffn_w_down):

    def _L0_attn_a_ref(x, norm_scale, in_w, in_b, conv_w, conv_b, xproj_w, dt_w, dt_b, A_log, D, out_w, out_b):
        import jax, jax.numpy as jnp
        import numpy as np
        B, T, H = (2, 256, 128)
        I, N, R, K = (256, 16, 64, 4)
        EPS = 1e-06
        Bsz, Tlen, Hd = x.shape
        Kk, Ii = conv_w.shape
        Nn = A_log.shape[1]
        Rr = dt_w.shape[0]
        xn = x * jax.lax.rsqrt(jnp.mean(x * x, axis=-1, keepdims=True) + EPS) * norm_scale
        proj = xn @ in_w + in_b
        hidden, gate = jnp.split(proj, 2, axis=-1)
        xp = jnp.pad(hidden, ((0, 0), (Kk - 1, 0), (0, 0)))
        conv = sum((conv_w[k] * xp[:, k:k + Tlen, :] for k in range(Kk))) + conv_b
        conv = jax.nn.silu(conv)
        xpj = conv @ xproj_w
        ts = xpj[..., :Rr]
        Bm = xpj[..., Rr:Rr + Nn]
        Cm = xpj[..., Rr + Nn:]
        delta = jax.nn.softplus(ts @ dt_w + dt_b)
        A = -jnp.exp(A_log)
        gate_a = jax.nn.silu(gate)

        def step(state, inp):
            h_t, d_t, g_t, B_t, C_t = inp
            dA = jnp.exp(A[None, :, :] * d_t[:, :, None])
            new = dA * state + d_t[:, :, None] * B_t[:, None, :] * h_t[:, :, None]
            y = jnp.einsum('bin,bn->bi', new, C_t) + D * h_t
            return (new, y * g_t)
        tm = lambda a: jnp.swapaxes(a, 0, 1)
        init = jnp.zeros((Bsz, Ii, Nn), x.dtype)
        _, ys = jax.lax.scan(step, init, (tm(conv), tm(delta), tm(gate_a), tm(Bm), tm(Cm)))
        ssm = jnp.swapaxes(ys, 0, 1)
        return ssm @ out_w + out_b

    def _L0_attn_b_ref(inputs, W_uv, b_uv, gamma, beta, W_out, b_out):
        import jax, jax.numpy as jnp
        import numpy as np
        H = 128
        E = 2 * H
        S_DIM = 128
        B, S = (4, 256)
        seq_len = inputs.shape[1]
        uvb = jax.nn.silu(jnp.einsum('bsh,hf->bsf', inputs, W_uv) + b_uv)
        u = uvb[..., :E]
        v = uvb[..., E:2 * E]
        base = uvb[..., 2 * E:]
        qk = base[..., None, :] * gamma + beta
        q, k = (qk[..., 0, :], qk[..., 1, :])
        scores = jnp.einsum('bns,bms->bnm', q, k) / seq_len
        sq = jnp.square(jax.nn.relu(scores))
        attn_v = jnp.einsum('bnm,bme->bne', sq, v)
        return jnp.einsum('bne,eh->bnh', u * attn_v, W_out) + b_out

    def _L0_ffn_ref(hidden_states, router_w, w_gate, w_up, w_down):
        import jax, jax.numpy as jnp
        import numpy as np
        NUM_EXPERTS = 8
        TOP_K = 2
        HIDDEN = 128
        INTER = 352

        def _moe_forward(hidden_states, router_w, w_gate, w_up, w_down):
            B, S, H = hidden_states.shape
            x = hidden_states.reshape(B * S, H)
            logits = x @ router_w
            probs = jax.nn.softmax(logits, axis=-1)
            top_vals, top_idx = jax.lax.top_k(probs, TOP_K)
            weights = top_vals / jnp.sum(top_vals, axis=-1, keepdims=True)
            out = jnp.zeros_like(x)
            for e in range(NUM_EXPERTS):
                w_e = jnp.sum(weights * (top_idx == e), axis=-1)
                gate_o = x @ w_gate[e]
                up_o = x @ w_up[e]
                inter = up_o * jax.nn.silu(gate_o)
                out = out + w_e[:, None] * (inter @ w_down[e])
            return out.reshape(B, S, H)
        return _moe_forward(hidden_states, router_w, w_gate, w_up, w_down)
    x = L0_attn_a_x
    x = x + _L0_attn_a_ref(_layernorm(x, axis=-1), L0_attn_a_norm_scale, L0_attn_a_in_w, L0_attn_a_in_b, L0_attn_a_conv_w, L0_attn_a_conv_b, L0_attn_a_xproj_w, L0_attn_a_dt_w, L0_attn_a_dt_b, L0_attn_a_A_log, L0_attn_a_D, L0_attn_a_out_w, L0_attn_a_out_b)
    x = x + _L0_ffn_ref(_layernorm(x, axis=-1), L0_ffn_router_w, L0_ffn_w_gate, L0_ffn_w_up, L0_ffn_w_down)
    x = x + _L0_attn_b_ref(_layernorm(x, axis=-1), L0_attn_b_W_uv, L0_attn_b_b_uv, L0_attn_b_gamma, L0_attn_b_beta, L0_attn_b_W_out, L0_attn_b_b_out)
    x = x + _L0_ffn_ref(_layernorm(x, axis=-1), L0_ffn_router_w, L0_ffn_w_gate, L0_ffn_w_up, L0_ffn_w_down)
    return x

_drawn_inputs = setup_inputs


def setup_inputs(seed=0):
    import zlib

    import numpy as np

    out = dict(_drawn_inputs(seed))
    spreads = {'L0_attn_a_norm_scale': (1.0, 0.6),
     'L0_attn_a_in_b': (0.0, 0.474),
     'L0_attn_a_conv_b': (0.0, 0.33),
     'L0_attn_a_D': (1.0, 0.6),
     'L0_attn_a_out_b': (0.0, 0.1),
     'L0_attn_b_b_uv': (0.0, 0.8),
     'L0_attn_b_beta': (0.0, 0.8),
     'L0_attn_b_b_out': (0.0, 2.0)}
    factors = {'L0_attn_a_conv_w': 5.409,
     'L0_attn_a_xproj_w': 8.0,
     'L0_attn_a_dt_w': 8.0,
     'L0_attn_a_dt_b': 8.0,
     'L0_attn_a_A_log': 8.0,
     'L0_attn_a_out_w': 3.191,
     'L0_attn_b_W_uv': 8.0,
     'L0_attn_b_gamma': 8.0,
     'L0_attn_b_W_out': 8.0}
    for name, (base, spread) in spreads.items():
        noise = np.random.default_rng([zlib.crc32(name.encode()), seed]).standard_normal(out[name].shape)
        drawn = base * np.exp(spread * noise) if base else spread * noise
        out[name] = jnp.asarray(drawn.astype(out[name].dtype))
    for name, factor in factors.items():
        out[name] = (out[name] * factor).astype(out[name].dtype)
    return out
```

```python
from contextlib import ExitStack

import concourse.bass as bass
from concourse import mybir

ALU = mybir.AluOpType
ACT = mybir.ActivationFunctionType
AX = mybir.AxisListType
F32 = mybir.dt.float32
F32R = mybir.dt.float32r
BF16 = mybir.dt.bfloat16
I32 = mybir.dt.int32
U32 = mybir.dt.uint32

P = 128
H = 128
SEQ = 256
NSEQ = 2
GT = SEQ * NSEQ
NC = GT // P
IT = 2
NS = 16
KC = 4
RK = 64
XP = RK + 2 * NS
NE = 8
FI = 352
NJ = NE * FI // P
RING = 4
RJ = RING * FI // P
NDA = 4
NST = 3
EPS = 1e-5
RMS_EPS = 1e-6

V_NS, V_INB, V_CW, V_CB, V_DTB, V_ALOG, V_D, V_OUTB = 0, 1, 5, 13, 15, 17, 49, 51
V_UVB, V_GAMMA, V_BETA, V_WOB, V_END = 52, 55, 57, 59, 60

SEMS = """
 d_vecs d_x d_inw d_xpw d_dtw d_outw d_gate d_up d_down d_uv d_vb d_wo d_rw d_out
 w_zero w_const w_sel w_A w_inhi w_inlo w_hi w_lo w_iota v_chain a_chain
 m_var m_rstd m_xm m_xt m_hi m_lo m_proj m_hid m_gate m_conv m_h m_xp m_ts m_sel m_dt m_z m_e m_u m_ln
 m_delta m_B m_C m_dA m_dbx m_scan m_p m_yacc m_yg m_out m_yT m_yt2 m_x1
 f_var f_rstd f_xm f_xt f_hi f_lo f_lg f_lgm f_pe f_G f_U f_silu f_stt f_tr f_tev f_dn f_oT f_ot f_x
 f_gp f_ga f_qk f_sc f_rl f_sq f_av f_ua f_go f_gT f_gt
""".split()


def blocks_ready(e):
    return (e + 1) * FI // P


def blocks_touching(e):
    return -(-(e + 1) * FI // P)


def build(nc, x, vecs, in_w, xproj_w, dt_w, out_w, gate_w, up_w, down_w, uv_w, v_b, wo_w, router_w, out):
    groups = x.shape[0] // GT
    with ExitStack() as ctx:
        def sb(name, shape, dt=F32):
            return ctx.enter_context(nc.sbuf_tensor(name, shape, dt))

        ps = ctx.enter_context(nc.psum_tensor("ps", [P, 8, 512], F32))
        s = {n: ctx.enter_context(nc.semaphore(n)) for n in SEMS}
        psB, psC, psD = ps[:, 0, :], ps[:, 1, :], ps[:, 2:4, :]
        psG, psU, psT, psO = ps[:, 4, :], ps[:, 5, :], ps[:, 6, :], ps[:, 7, :]

        ident = sb("ident", [P, P])
        sel = sb("sel", [96, 2 * NS, P], BF16)
        ones_row = sb("ones_row", [1, P])
        neghalf = sb("neghalf", [P, NC])
        iota_i = sb("iota_i", [P, NE], I32)
        iota8 = sb("iota8", [P, NE])
        vec = sb("vec", [P, V_END])
        A = sb("A", [P, IT, NS])
        inw_raw = sb("inw_raw", [P, 512])
        inw_hi = sb("inw_hi", [P, 512], F32R)
        inw_lo = sb("inw_lo", [P, 512], F32R)
        xpw = sb("xpw", [P, IT, XP])
        dtw = sb("dtw", [RK, IT * P])
        outw = sb("outw", [P, IT, H])
        gate_hi = sb("gate_hi", [P, NE * FI], F32R)
        gate_lo = sb("gate_lo", [P, NE * FI], F32R)
        up_hi = sb("up_hi", [P, NE * FI], F32R)
        up_lo = sb("up_lo", [P, NE * FI], F32R)
        down = sb("down", [P, NJ, H])
        uv_hi = sb("uv_hi", [P, 640], F32R)
        uv_lo = sb("uv_lo", [P, 640], F32R)
        vb_row = sb("vb_row", [1, 2 * P])
        wo = sb("wo", [P, 2, H])
        rw_hi = sb("rw_hi", [P, NE], F32R)
        rw_lo = sb("rw_lo", [P, NE], F32R)

        xin = sb("xin", [P, NC, H])
        m_bn = sb("m_bn", [P, NC, 6])
        m_mv = sb("m_mv", [P, NC, 2])
        m_ve = sb("m_ve", [P, NC])
        m_r = sb("m_r", [P, NC])
        m_xn = sb("m_xn", [P, NC, H])
        m_xhi = sb("m_xhi", [P, GT], F32R)
        m_xlo = sb("m_xlo", [P, GT], F32R)
        xpad = sb("xpad", [P, IT, NSEQ, SEQ + KC - 1])
        h = sb("h", [P, IT, GT])
        gact = sb("gact", [P, IT, GT])
        ts = sb("ts", [RK, GT])
        bc_f = sb("bc_f", [96, GT])
        bc_r = sb("bc_r", [96, GT])
        bc_2 = sb("bc_2", [96, GT], BF16)
        bc_3 = sb("bc_3", [96, GT], BF16)
        bc_s = sb("bc_s", [96, GT], BF16)
        delta = sb("delta", [P, IT, GT])
        dx = sb("dx", [P, IT, GT])
        dA = sb("dA", [P, NDA, IT, NSEQ, SEQ])
        st = sb("st", [P, NST, IT, GT])
        yacc = sb("yacc", [P, IT, GT])
        yT = sb("yT", [P, GT])
        x1 = sb("x1", [P, NC, H])
        conv = delta
        sp_z, sp_e, sp_u, sp_c = yacc, st[:, 0], st[:, 1], st[:, 2]
        sp_ln = dx

        f_bn = sb("f_bn", [P, NC, 6])
        f_mv = sb("f_mv", [P, NC, 2])
        f_ve = sb("f_ve", [P, NC])
        f_r = sb("f_r", [P, NC])
        f_xn = sb("f_xn", [P, NC, H])
        xhi = sb("xhi", [P, GT], F32R)
        xlo = sb("xlo", [P, GT], F32R)
        lg_mx = sb("lg_mx", [P, NC])
        lg = sb("lg", [P, NC, NE])
        pe_ = sb("pe_", [P, NC, NE])
        prob = sb("prob", [P, NC, NE])
        psum_ = sb("psum_", [P, NC])
        prec = sb("prec", [P, NC])
        top8 = sb("top8", [P, NC, 8])
        idx8 = sb("idx8", [P, NC, 8], U32)
        idxf = sb("idxf", [P, NC, 2])
        den = sb("den", [P, NC])
        rden = sb("rden", [P, NC])
        w2 = sb("w2", [P, NC, 2])
        m1 = sb("m1", [P, NC, NE])
        m2 = sb("m2", [P, NC, NE])
        wts = sb("wts", [P, NC, NE])
        sl = sb("sl", [P, 2, FI])
        inner = sb("inner", [P, NC, RING * FI])
        innerT = sb("innerT", [P, 2, GT])
        outT = sb("outT", [P, GT])
        x2 = sb("x2", [P, NC, H])
        x3 = sb("x3", [P, NC, H])
        flat = inner[:].rearrange("p c j -> p (c j)")
        raw_gate, raw_up = flat[:, 0:NE * FI], flat[:, NE * FI:2 * NE * FI]
        raw_uv = sl[:].rearrange("p a j -> p (a j)")[:, 0:640]
        raw_rw = sl[:].rearrange("p a j -> p (a j)")[:, 640:640 + NE]
        at_base, at_q, at_k = (flat[:, i * GT:(i + 1) * GT] for i in range(3))
        at_u = flat[:, 3 * GT:5 * GT].rearrange("p (a t) -> p a t", a=2)
        at_v = flat[:, 5 * GT:7 * GT].rearrange("p (c e) -> p c e", c=NC)
        at_s = flat[:, 7 * GT:9 * GT].rearrange("p (b t) -> p b t", b=2)
        at_ua = flat[:, 9 * GT:11 * GT].rearrange("p (a t) -> p a t", a=2)

        def v(col, n=1):
            return vec[:, col:col + n]

        def chunks(bank):
            return bank.rearrange("p (c t) -> p c t", c=NC)

        def block_of(schedule, ingroup, outgroup, first):
            block = ctx2.enter_context(nc.Block())

            @block.sync
            def _(sp):
                if first:
                    sp.dma_start(vec[:], vecs).then_inc(s["d_vecs"], 16)
                if ingroup is not None:
                    rows = x[bass.ds(ingroup * GT, GT), :]
                    sp.dma_start(xin[:], rows.rearrange("(c p) h -> p c h", p=P)).then_inc(s["d_x"], 16)
                if first:
                    for sem, dst, src in ((s["d_inw"], inw_raw[:], in_w), (s["d_xpw"], xpw[:], xproj_w),
                                          (s["d_dtw"], dtw[:], dt_w), (s["d_outw"], outw[:], out_w),
                                          (s["d_gate"], raw_gate, gate_w), (s["d_up"], raw_up, up_w),
                                          (s["d_uv"], raw_uv, uv_w), (s["d_rw"], raw_rw, router_w),
                                          (s["d_down"], down[:], down_w), (s["d_vb"], vb_row[:], v_b),
                                          (s["d_wo"], wo[:], wo_w)):
                        sp.dma_start(dst, src).then_inc(sem, 16)
                    sp.wait_ge(s["d_down"], 16)
                    sp.wait_ge(s["d_vb"], 16)
                    sp.wait_ge(s["d_wo"], 16)
                if outgroup is not None:
                    sp.wait_ge(s["f_x"], 3)
                    rows = out[bass.ds(outgroup * GT, GT), :]
                    sp.dma_start(rows.rearrange("(c p) h -> p c h", p=P), x3[:]).then_inc(s["d_out"], 16)
                    sp.wait_ge(s["d_out"], 16)

            @block.gpsimd
            def _(pool):
                def setup(_):
                    nc.gpsimd.memset(ident[:], 0.0).then_inc(s["w_zero"], 1)
                    nc.gpsimd.memset(sel[:], 0.0).then_inc(s["w_zero"], 1)
                    nc.gpsimd.memset(ones_row[:], 1.0)
                    nc.gpsimd.memset(neghalf[:], -0.5)
                    nc.gpsimd.iota(iota_i[:], pattern=[[1, NE]], base=0, channel_multiplier=0).then_inc(s["w_iota"], 1)
                    pool.wait_ge(s["w_zero"], 2)
                    nc.gpsimd.affine_select(out=ident[:], in_=ident[:], compare_op=ALU.not_equal, fill=1.0, base=0,
                                            pattern=[[-1, P]], channel_multiplier=1).then_inc(s["w_const"], 1)
                    pool.wait_ge(s["w_const"], 1)
                    for q in range(3):
                        if q:
                            pool.wait_ge(s["w_sel"], q)
                        part = sel[32 * q:32 * q + 32, :, :]
                        nc.gpsimd.affine_select(out=part, in_=part, compare_op=ALU.not_equal, fill=1.0, base=0,
                                                pattern=[[-1, 2 * NS], [0, P]],
                                                channel_multiplier=1).then_inc(s["w_sel"], 1)
                    pool.wait_ge(s["w_sel"], 3)

                def split_weights(_):
                    for n, (lo, raw, hi) in enumerate(((gate_lo[:], raw_gate, gate_hi[:]), (up_lo[:], raw_up, up_hi[:]),
                                                       (uv_lo[:], raw_uv, uv_hi[:]), (rw_lo[:], raw_rw, rw_hi[:]))):
                        pool.wait_ge(s["w_hi"], n + 1)
                        nc.gpsimd.tensor_tensor(lo, raw, hi.bitcast(F32), ALU.subtract).then_inc(s["w_lo"], 1)

                def m_rstd(_):
                    pool.wait_ge(s["m_var"], 1)
                    nc.gpsimd.tensor_tensor(m_r[:], m_ve[:], neghalf[:], ALU.pow).then_inc(s["m_rstd"], 1)

                def f_rstd(k):
                    pool.wait_ge(s["f_var"], k + 1)
                    nc.gpsimd.tensor_tensor(f_r[:], f_ve[:], neghalf[:], ALU.pow).then_inc(s["f_rstd"], 1)

                def unit(n):
                    if n == 0:
                        return
                    pool.wait_ge(s["m_p"], n + 1)
                    if n > 1:
                        pool.wait_ge(s["m_yacc"], n - 1)
                    nc.gpsimd.tensor_tensor(yacc[:], st[:, 0] if n == 1 else yacc[:], st[:, n % NST],
                                            ALU.add).then_inc(s["m_yacc"], 1)

                run = {"setup": setup, "split_weights": split_weights, "m_ln": m_rstd, "f_ln": f_rstd, "unit": unit}
                for step, k in schedule:
                    if step in run:
                        run[step](k)

            @block.scalar
            def _(act):
                chain = [0]

                def link(ins):
                    chain[0] += 1
                    ins.then_inc(s["a_chain"], 1)
                    act.wait_ge(s["a_chain"], chain[0])

                def setup(_):
                    act.wait_ge(s["d_vecs"], 16)
                    nc.scalar.activation(A[:].rearrange("p a n -> p (a n)"), v(V_ALOG, IT * NS), ACT.Exp).then_inc(s["w_A"], 1)
                    act.wait_ge(s["d_inw"], 16)
                    nc.scalar.copy(inw_hi[:], inw_raw[:]).then_inc(s["w_inhi"], 1)

                def split_weights(_):
                    for sem, raw, hi in ((s["d_gate"], raw_gate, gate_hi[:]), (s["d_up"], raw_up, up_hi[:]),
                                         (s["d_uv"], raw_uv, uv_hi[:]), (s["d_rw"], raw_rw, rw_hi[:])):
                        act.wait_ge(sem, 16)
                        nc.scalar.copy(hi, raw).then_inc(s["w_hi"], 1)

                def m_xt(_):
                    act.wait_ge(s["m_xt"], 1)
                    nc.scalar.activation(m_xhi[:], psB, ACT.Copy, scale=v(V_NS)).then_inc(s["m_hi"], 1)

                def m_proj(_):
                    for it in range(IT):
                        act.wait_ge(s["m_proj"], it + 1)
                        bank = (psC, psD[:, 0, :])[it]
                        nc.scalar.activation(xpad[:, it, :, KC - 1:], bank.rearrange("p (b t) -> p b t", b=NSEQ),
                                             ACT.Identity, bias=v(V_INB + it)).then_inc(s["m_hid"], 1)
                    for it in range(IT):
                        act.wait_ge(s["m_proj"], IT + it + 1)
                        bank = (psD[:, 1, :], psB)[it]
                        nc.scalar.activation(gact[:, it, :], bank, ACT.Silu, bias=v(V_INB + IT + it)).then_inc(s["m_gate"], 1)

                def m_conv(_):
                    for it in range(IT):
                        act.wait_ge(s["m_conv"], it + 1)
                        nc.scalar.activation(h[:, it, :], conv[:, it, :], ACT.Silu).then_inc(s["m_h"], 1)

                def m_xproj(_):
                    act.wait_ge(s["m_xp"], 1)
                    nc.scalar.copy(bc_f[64:96, :], psC[64:96, :]).then_inc(s["m_ts"], 1)
                    nc.scalar.copy(ts[:], psC[0:RK, :]).then_inc(s["m_ts"], 1)

                def m_softplus(_):
                    for it in range(IT):
                        act.wait_ge(s["m_dt"], it + 1)
                        nc.scalar.activation(sp_e[:, it, :], psD[:, it, :], ACT.Abs, bias=v(V_DTB + it)).then_inc(s["a_chain"], 1)
                        chain[0] += 1
                        nc.scalar.activation(sp_z[:, it, :], psD[:, it, :], ACT.Identity, bias=v(V_DTB + it)).then_inc(s["m_z"], 1)
                    act.wait_ge(s["a_chain"], chain[0])
                    act.preload_act_table_set("natural_log_exp_and_others")
                    nc.scalar.activation(sp_e, sp_e, ACT.Exp, scale=-1.0).then_inc(s["m_e"], 1)
                    act.wait_ge(s["m_u"], 1)
                    nc.scalar.activation(sp_ln[:], sp_u, ACT.Ln).then_inc(s["m_ln"], 1)

                def decays(j):
                    for n in range(NDA * j, NDA * j + NDA):
                        act.wait_ge(s["m_delta"], 1)
                        if n >= NDA:
                            act.wait_ge(s["m_scan"], n - NDA + 1)
                        for it in range(IT):
                            src = delta[:, it, :].rearrange("p (b t) -> p b t", b=NSEQ)
                            ins = nc.scalar.activation(dA[:, n % NDA, it, :, 1:], src[:, :, 1:], ACT.Exp,
                                                       scale=A[:, it, n:n + 1])
                        ins.then_inc(s["m_dA"], 1)

                def m_out(_):
                    act.wait_ge(s["m_out"], 1)
                    nc.scalar.activation(yT[:], psB, ACT.Identity, bias=v(V_OUTB)).then_inc(s["m_yT"], 1)

                def f_xt(k):
                    act.wait_ge(s["f_xt"], k + 1)
                    nc.scalar.copy(xhi[:], psT).then_inc(s["f_hi"], 1)

                def route(m):
                    act.wait_ge(s["f_lgm"], m + 1)
                    nc.scalar.activation(pe_[:], lg[:], ACT.Exp).then_inc(s["f_pe"], 1)

                def silu(i):
                    act.wait_ge(s["f_G"], i + 1)
                    if i >= 2:
                        act.wait_ge(s["f_stt"], i - 1)
                    nc.scalar.activation(sl[:, i % 2, :], psG[:, 0:FI], ACT.Silu).then_inc(s["f_silu"], 1)

                def evac(b):
                    act.wait_ge(s["f_tr"], b + 1)
                    if b >= 2:
                        act.wait_ge(s["f_dn"], b - 1)
                    nc.scalar.copy(innerT[:, b % 2, :], psT).then_inc(s["f_tev"], 1)

                def moe(me):
                    m, e = divmod(me, NE)
                    todo = blocks_of(m, e - 1)
                    for c in range(NC):
                        silu(me * NC + c)
                        if c < len(todo):
                            evac(todo[c])

                def moe_end(m):
                    for b in blocks_of(m, NE - 1):
                        evac(b)
                    act.wait_ge(s["f_dn"], NJ * (m + 1))
                    nc.scalar.copy(outT[:], psO).then_inc(s["f_oT"], 1)

                def at_proj(_):
                    act.wait_ge(s["f_gp"], 1)
                    nc.scalar.activation(at_base, psO, ACT.Silu, bias=v(V_UVB + 2)).then_inc(s["f_ga"], 1)
                    for a, bank in ((0, psG), (1, psU)):
                        act.wait_ge(s["f_gp"], 2 + a)
                        nc.scalar.activation(at_u[:, a, :], bank, ACT.Silu, bias=v(V_UVB + a)).then_inc(s["f_ga"], 1)
                    for a, bank in ((0, psT), (1, psO)):
                        act.wait_ge(s["f_gp"], 4 + a)
                        nc.scalar.activation(at_v[:, 2 * a:2 * a + 2, :], bank.rearrange("p (c e) -> p c e", c=2),
                                             ACT.Silu).then_inc(s["f_ga"], 1)

                def at_scores(_):
                    for b, bank in ((0, psG), (1, psU)):
                        act.wait_ge(s["f_sc"], b + 1)
                        nc.scalar.activation(at_s[:, b, :], bank, ACT.Relu, scale=1.0 / SEQ).then_inc(s["f_rl"], 1)

                def at_out(_):
                    act.wait_ge(s["f_go"], 1)
                    nc.scalar.activation(outT[:], psG, ACT.Identity, bias=v(V_WOB)).then_inc(s["f_gT"], 1)

                run = {"setup": setup, "split_weights": split_weights, "m_xt": m_xt, "m_proj": m_proj,
                       "m_conv": m_conv, "m_xproj": m_xproj, "m_softplus": m_softplus, "decays": decays,
                       "m_out": m_out, "f_xt": f_xt, "route": route, "moe": moe, "moe_end": moe_end,
                       "at_proj": at_proj, "at_scores": at_scores, "at_out": at_out}
                for step, k in schedule:
                    if step in run:
                        run[step](k)

            @block.vector
            def _(dve):
                chain = [0]

                def mark(ins):
                    chain[0] += 1
                    ins.then_inc(s["v_chain"], 1)

                def link():
                    dve.wait_ge(s["v_chain"], chain[0])

                def setup(_):
                    for it in range(IT):
                        nc.vector.memset(xpad[:, it, :, 0:KC - 1], 0.0)
                    for n in range(NDA):
                        nc.vector.memset(dA[:, n, :, :, 0:1].rearrange("p a b o -> p (a b) o"), 0.0)
                    dve.wait_ge(s["w_iota"], 1)
                    mark(nc.vector.tensor_copy(iota8[:], iota_i[:]))
                    dve.wait_ge(s["w_A"], 1)
                    a = A[:].rearrange("p a n -> p (a n)")
                    nc.vector.tensor_scalar(a, a, -1.0, None, ALU.mult).then_inc(s["w_A"], 1)
                    dve.wait_ge(s["w_inhi"], 1)
                    nc.vector.tensor_tensor(inw_lo[:], inw_raw[:], inw_hi[:].bitcast(F32), ALU.subtract).then_inc(s["w_inlo"], 1)

                def norm_stats(xt, bn, mv):
                    for c in range(NC):
                        mark(nc.vector.bn_stats(bn[:, c, :], xt[:, c, :]))
                    link()
                    for c in range(NC):
                        mark(nc.vector.bn_aggr(mv[:, c, :], bn[:, c, :]))
                    link()

                def m_ln(_):
                    dve.wait_ge(s["d_x"], 16)
                    norm_stats(xin, m_bn, m_mv)
                    nc.vector.tensor_scalar(m_ve[:], m_mv[:, :, 1], 1.0 + RMS_EPS, RMS_EPS * EPS,
                                            ALU.mult, ALU.add).then_inc(s["m_var"], 1)

                def m_norm(_):
                    dve.wait_ge(s["m_rstd"], 1)
                    for c in range(NC):
                        ins = nc.vector.tensor_scalar(m_xn[:, c, :], xin[:, c, :], m_mv[:, c, 0:1], m_r[:, c:c + 1],
                                                      ALU.subtract, ALU.mult)
                    ins.then_inc(s["m_xm"], 1)

                def m_xt(_):
                    dve.wait_ge(s["m_hi"], 1)
                    nc.vector.scalar_tensor_tensor(out=m_xlo[:], in0=psB, scalar=v(V_NS), in1=m_xhi[:].bitcast(F32),
                                                   op0=ALU.mult, op1=ALU.subtract).then_inc(s["m_lo"], 1)

                def m_conv(_):
                    for k in range(KC):
                        if k:
                            link()
                        for it in range(IT):
                            w = v(V_CW + it * KC + k)
                            src = xpad[:, it, :, k:k + SEQ]
                            dst = conv[:, it, :].rearrange("p (b t) -> p b t", b=NSEQ)
                            if k == 0:
                                dve.wait_ge(s["m_hid"], it + 1)
                                mark(nc.vector.tensor_scalar(dst, src, w, v(V_CB + it), ALU.mult, ALU.add))
                            else:
                                ins = nc.vector.scalar_tensor_tensor(out=dst, in0=src, scalar=w, in1=dst,
                                                                     op0=ALU.mult, op1=ALU.add)
                                if k < KC - 1:
                                    mark(ins)
                                else:
                                    ins.then_inc(s["m_conv"], 1)

                def m_split(_):
                    dve.wait_ge(s["m_ts"], 1)
                    mark(nc.vector.tensor_copy(bc_s[64:96, :], bc_f[64:96, :]))
                    link()
                    mark(nc.vector.tensor_tensor(bc_r[64:96, :], bc_f[64:96, :], bc_s[64:96, :], ALU.subtract))
                    link()
                    mark(nc.vector.tensor_copy(bc_2[64:96, :], bc_r[64:96, :]))
                    link()
                    mark(nc.vector.tensor_tensor(bc_3[64:96, :], bc_r[64:96, :], bc_2[64:96, :], ALU.subtract))
                    nc.vector.tensor_copy(bc_s[32:64, :], bc_2[64:96, :]).then_inc(s["m_sel"], 1)
                    link()
                    nc.vector.tensor_copy(bc_s[0:32, :], bc_3[64:96, :]).then_inc(s["m_sel"], 1)

                def m_softplus(_):
                    dve.wait_ge(s["m_e"], 1)
                    nc.vector.tensor_scalar(sp_u, sp_e, 1.0, None, ALU.add).then_inc(s["m_u"], 1)
                    dve.wait_ge(s["m_u"], 1)
                    mark(nc.vector.scalar_tensor_tensor(out=sp_c, in0=sp_u, scalar=-1.0, in1=sp_e,
                                                        op0=ALU.add, op1=ALU.subtract))
                    link()
                    dve.wait_ge(s["m_ln"], 1)
                    mark(nc.vector.tensor_tensor(sp_c, sp_ln[:], sp_c, ALU.subtract))
                    link()
                    dve.wait_ge(s["m_z"], 2)
                    nc.vector.scalar_tensor_tensor(out=delta[:], in0=sp_z[:], scalar=0.0, in1=sp_c,
                                                   op0=ALU.max, op1=ALU.add).then_inc(s["m_delta"], 1)
                    dve.wait_ge(s["m_delta"], 1)
                    mark(nc.vector.tensor_tensor(dx[:], delta[:], h[:], ALU.mult))
                    link()

                def times_C(n):
                    dve.wait_ge(s["m_C"], n + 1)
                    dve.wait_ge(s["m_scan"], n + 1)
                    nc.vector.tensor_tensor(st[:, n % NST], st[:, n % NST], psC.unsqueeze(1).broadcast_to([P, IT, GT]),
                                            ALU.mult).then_inc(s["m_p"], 1)

                def unit(n):
                    dve.wait_ge(s["m_B"], n + 1)
                    if n:
                        dve.wait_ge(s["m_scan"], n)
                    nc.vector.tensor_tensor(psD, dx[:], psB.unsqueeze(1).broadcast_to([P, IT, GT]),
                                            ALU.mult).then_inc(s["m_dbx"], 1)
                    if n:
                        times_C(n - 1)
                    dve.wait_ge(s["m_dA"], n + 1)
                    dve.wait_ge(s["m_dbx"], n + 1)
                    if n >= NST:
                        dve.wait_ge(s["m_yacc"], max(1, n - NST))
                    nc.vector.tensor_tensor_scan(out=st[:, n % NST].rearrange("p a t -> p (a t)"),
                                                 data0=dA[:, n % NDA].rearrange("p a b t -> p (a b t)"),
                                                 data1=psD.rearrange("p a t -> p (a t)"), initial=0.0,
                                                 op0=ALU.mult, op1=ALU.add).then_inc(s["m_scan"], 1)
                    if n == NS - 1:
                        times_C(n)

                def m_gate(_):
                    dve.wait_ge(s["m_yacc"], NS - 1)
                    for it in range(IT):
                        mark(nc.vector.scalar_tensor_tensor(out=yacc[:, it, :], in0=h[:, it, :], scalar=v(V_D + it),
                                                            in1=yacc[:, it, :], op0=ALU.mult, op1=ALU.add))
                    link()
                    nc.vector.tensor_tensor(yacc[:], yacc[:], gact[:], ALU.mult).then_inc(s["m_yg"], 1)

                def m_res(_):
                    dve.wait_ge(s["m_yt2"], 1)
                    nc.vector.tensor_tensor(x1[:], xin[:], chunks(psC), ALU.add).then_inc(s["m_x1"], 1)

                def f_ln(k):
                    xt = (x1, x2, x2)[k]
                    if k:
                        dve.wait_ge(s["f_x"], k)
                    norm_stats(xt, f_bn, f_mv)
                    nc.vector.tensor_scalar(f_ve[:], f_mv[:, :, 1], EPS, None, ALU.add).then_inc(s["f_var"], 1)

                def f_norm(k):
                    xt = (x1, x2, x2)[k]
                    dve.wait_ge(s["f_rstd"], k + 1)
                    if k:
                        dve.wait_ge(s["f_xt"], k)
                    for c in range(NC):
                        ins = nc.vector.tensor_scalar(f_xn[:, c, :], xt[:, c, :], f_mv[:, c, 0:1], f_r[:, c:c + 1],
                                                      ALU.subtract, ALU.mult)
                    ins.then_inc(s["f_xm"], 1)

                def f_xt(k):
                    dve.wait_ge(s["f_hi"], k + 1)
                    nc.vector.tensor_tensor(xlo[:], psT, xhi[:].bitcast(F32), ALU.subtract).then_inc(s["f_lo"], 1)

                def col(a, j):
                    return a[:, :, j:j + 1]

                def wide(a, n):
                    return a[:].unsqueeze(2).broadcast_to([P, NC, n])

                def route(m):
                    dve.wait_ge(s["f_lg"], m + 1)
                    lgp = psU[:, 0:NC * NE].rearrange("p (c e) -> p c e", c=NC)
                    mark(nc.vector.reduce_max(lg_mx[:], lgp, AX.X))
                    link()
                    nc.vector.tensor_tensor(lg[:], lgp, wide(lg_mx, NE), ALU.subtract).then_inc(s["f_lgm"], 1)

                def top2(m):
                    dve.wait_ge(s["f_pe"], m + 1)
                    mark(nc.vector.tensor_reduce(psum_[:], pe_[:], AX.X, ALU.add))
                    link()
                    mark(nc.vector.reciprocal(prec[:], psum_[:]))
                    link()
                    mark(nc.vector.tensor_tensor(prob[:], pe_[:], wide(prec, NE), ALU.mult))
                    link()
                    for c in range(NC):
                        mark(nc.vector.max(top8[:, c, :], prob[:, c, :]))
                    link()
                    for c in range(NC):
                        mark(nc.vector.max_index(idx8[:, c, :], top8[:, c, :], prob[:, c, :]))
                    mark(nc.vector.tensor_tensor(den[:], top8[:, :, 0], top8[:, :, 1], ALU.add))
                    link()
                    mark(nc.vector.tensor_copy(idxf[:], idx8[:, :, 0:2]))
                    mark(nc.vector.reciprocal(rden[:], den[:]))
                    link()
                    mark(nc.vector.tensor_tensor(w2[:], top8[:, :, 0:2], wide(rden, 2), ALU.mult))
                    link()
                    for c in range(NC):
                        for j, mk in ((0, m1), (1, m2)):
                            mark(nc.vector.tensor_scalar(mk[:, c, :], iota8[:], idxf[:, c, j:j + 1], w2[:, c, j:j + 1],
                                                         ALU.is_equal, ALU.mult))
                    link()
                    mark(nc.vector.tensor_tensor(wts[:], m1[:], m2[:], ALU.add))
                    link()

                def moe(me):
                    m, e = divmod(me, NE)
                    for c in range(NC):
                        i = me * NC + c
                        dve.wait_ge(s["f_silu"], i + 1)
                        dve.wait_ge(s["f_U"], i + 1)
                        if e >= RING and c == 0:
                            dve.wait_ge(s["f_tr"], NJ * m + blocks_touching(e - RING))
                        at = (e % RING) * FI
                        nc.vector.scalar_tensor_tensor(out=inner[:, c, at:at + FI], in0=sl[:, i % 2, :],
                                                       scalar=wts[:, c, e:e + 1], in1=psU[:, 0:FI],
                                                       op0=ALU.mult, op1=ALU.mult).then_inc(s["f_stt"], 1)

                def moe_res(m):
                    dve.wait_ge(s["f_ot"], m + 1)
                    old, new = ((x1, x2), (x2, x3))[m]
                    if m:
                        dve.wait_ge(s["f_x"], 2)
                    nc.vector.tensor_tensor(new[:], old[:], chunks(psT), ALU.add).then_inc(s["f_x"], 1)

                def at_proj(_):
                    dve.wait_ge(s["f_ga"], 1)
                    for j, dst in ((0, at_q), (1, at_k)):
                        nc.vector.tensor_scalar(dst, at_base, v(V_GAMMA + j), v(V_BETA + j),
                                                ALU.mult, ALU.add).then_inc(s["f_qk"], 1)

                def at_scores(_):
                    for b in range(2):
                        dve.wait_ge(s["f_rl"], b + 1)
                        nc.vector.tensor_tensor(at_s[:, b, :], at_s[:, b, :], at_s[:, b, :], ALU.mult).then_inc(s["f_sq"], 1)

                def at_mix(_):
                    for a, bank in ((0, psT), (1, psO)):
                        dve.wait_ge(s["f_av"], a + 1)
                        nc.vector.tensor_tensor(at_ua[:, a, :], at_u[:, a, :], bank, ALU.mult).then_inc(s["f_ua"], 1)

                def at_res(_):
                    dve.wait_ge(s["f_gt"], 1)
                    nc.vector.tensor_tensor(x2[:], x2[:], chunks(psU), ALU.add).then_inc(s["f_x"], 1)

                run = {"setup": setup, "m_ln": m_ln, "m_norm": m_norm, "m_xt": m_xt, "m_conv": m_conv,
                       "m_xproj": m_split, "m_softplus": m_softplus, "unit": unit, "m_gate": m_gate,
                       "m_res": m_res, "f_ln": f_ln, "f_norm": f_norm, "f_xt": f_xt, "route": route,
                       "top2": top2, "moe": moe, "moe_res": moe_res, "at_proj": at_proj,
                       "at_scores": at_scores, "at_mix": at_mix, "at_res": at_res}
                for step, k in schedule:
                    if step in run:
                        run[step](k)

            @block.tensor
            def _(pe):
                def transposes(bank, src):
                    for c in range(NC):
                        ins = nc.tensor.transpose(bank[:, c * P:(c + 1) * P], src(c), ident[:])
                    return ins

                def three(bank, w, xs, first=True, last=True):
                    nc.tensor.matmul(bank, w[0], xs[0], start=first, stop=False)
                    nc.tensor.matmul(bank, w[0], xs[1], start=False, stop=False)
                    return nc.tensor.matmul(bank, w[1], xs[0], start=False, stop=last)

                def m_norm(_):
                    if first:
                        pe.wait_ge(s["w_const"], 1)
                    pe.wait_ge(s["m_xm"], 1)
                    transposes(psB, lambda c: m_xn[:, c, :]).then_inc(s["m_xt"], 1)

                def m_proj(_):
                    if first:
                        pe.wait_ge(s["w_inlo"], 1)
                    pe.wait_ge(s["m_lo"], 1)
                    for j, bank in enumerate((psC, psD[:, 0, :], psD[:, 1, :], psB)):
                        cols = slice(j * P, (j + 1) * P)
                        three(bank, (inw_hi[:, cols], inw_lo[:, cols]), (m_xhi[:], m_xlo[:])).then_inc(s["m_proj"], 1)

                def m_xproj(_):
                    if first:
                        pe.wait_ge(s["d_xpw"], 16)
                    pe.wait_ge(s["m_hid"], 1)
                    for it in range(IT):
                        pe.wait_ge(s["m_h"], it + 1)
                        ins = nc.tensor.matmul(psC[0:XP, :], xpw[:, it, :], h[:, it, :], start=it == 0, stop=it == IT - 1)
                    ins.then_inc(s["m_xp"], 1)

                def m_dt(_):
                    if first:
                        pe.wait_ge(s["d_dtw"], 16)
                    pe.wait_ge(s["m_ts"], 2)
                    pe.wait_ge(s["m_hid"], 2)
                    pe.wait_ge(s["m_gate"], 1)
                    for it in range(IT):
                        nc.tensor.matmul(psD[:, it, :], dtw[:, it * P:(it + 1) * P], ts[:], start=True,
                                         stop=True).then_inc(s["m_dt"], 1)

                def unit(n):
                    if n == 0:
                        if first:
                            pe.wait_ge(s["w_sel"], 3)
                        pe.wait_ge(s["m_sel"], 2)
                        pe.wait_ge(s["m_gate"], 2)
                    else:
                        pe.wait_ge(s["m_dbx"], n)
                    nc.tensor.matmul(psB, sel[:, n, :], bc_s[:], start=True, stop=True).then_inc(s["m_B"], 1)
                    if n:
                        pe.wait_ge(s["m_p"], n)
                    nc.tensor.matmul(psC, sel[:, NS + n, :], bc_s[:], start=True, stop=True).then_inc(s["m_C"], 1)

                def m_out(_):
                    if first:
                        pe.wait_ge(s["d_outw"], 16)
                    pe.wait_ge(s["m_yg"], 1)
                    for it in range(IT):
                        ins = nc.tensor.matmul(psB, outw[:, it, :], yacc[:, it, :], start=it == 0, stop=it == IT - 1)
                    ins.then_inc(s["m_out"], 1)
                    pe.wait_ge(s["m_yT"], 1)
                    transposes(psC, lambda c: yT[:, c * P:(c + 1) * P]).then_inc(s["m_yt2"], 1)

                def f_norm(k):
                    pe.wait_ge(s["f_xm"], k + 1)
                    transposes(psT, lambda c: f_xn[:, c, :]).then_inc(s["f_xt"], 1)

                def route(m):
                    pe.wait_ge(s["f_lo"], (1, 3)[m])
                    for c in range(NC):
                        cols = slice(c * P, (c + 1) * P)
                        ins = three(psU[:, c * NE:(c + 1) * NE], (xhi[:, cols], xlo[:, cols]), (rw_hi[:], rw_lo[:]))
                    ins.then_inc(s["f_lg"], 1)

                def turn(b):
                    if b % NJ:
                        pe.wait_ge(s["f_tev"], b)
                    at = (b % NJ % RJ) * P
                    transposes(psT, lambda c: inner[:, c, at:at + P]).then_inc(s["f_tr"], 1)

                def lower(b):
                    pe.wait_ge(s["f_tev"], b + 1)
                    nc.tensor.matmul(psO, down[:, b % NJ, :], innerT[:, b % 2, :], start=b % NJ == 0,
                                     stop=b % NJ == NJ - 1).then_inc(s["f_dn"], 1)

                def moe(me):
                    m, e = divmod(me, NE)
                    todo = blocks_of(m, e - 1)
                    for c in range(NC):
                        i = me * NC + c
                        cols, wcols = slice(c * P, (c + 1) * P), slice(e * FI, (e + 1) * FI)
                        xs = (xhi[:, cols], xlo[:, cols])
                        if i:
                            pe.wait_ge(s["f_silu"], i)
                        three(psG[:, 0:FI], xs, (gate_hi[:, wcols], gate_lo[:, wcols])).then_inc(s["f_G"], 1)
                        if i % (NE * NC):
                            pe.wait_ge(s["f_stt"], i)
                        else:
                            pe.wait_ge(s["f_lgm"], m + 1)
                        three(psU[:, 0:FI], xs, (up_hi[:, wcols], up_lo[:, wcols])).then_inc(s["f_U"], 1)
                        if c and c - 1 < len(todo):
                            lower(todo[c - 1])
                        if c < len(todo):
                            if c == 0:
                                pe.wait_ge(s["f_stt"], me * NC)
                            turn(todo[c])

                def moe_end(m):
                    pe.wait_ge(s["f_stt"], (m + 1) * NE * NC)
                    for b in blocks_of(m, NE - 1):
                        turn(b)
                        lower(b)
                    pe.wait_ge(s["f_oT"], m + 1)
                    transposes(psT, lambda c: outT[:, c * P:(c + 1) * P]).then_inc(s["f_ot"], 1)

                def at_proj(_):
                    xs = (xhi[:], xlo[:])
                    pe.wait_ge(s["f_lo"], 2)
                    pe.wait_ge(s["f_silu"], NE * NC)
                    for bank, at in ((psO, 4), (psG, 0), (psU, 1)):
                        cols = slice(at * P, (at + 1) * P)
                        three(bank, (uv_hi[:, cols], uv_lo[:, cols]), xs).then_inc(s["f_gp"], 1)
                    for a, bank in ((0, psT), (1, psO)):
                        if a:
                            pe.wait_ge(s["f_ga"], 1)
                        for c in range(2 * a, 2 * a + 2):
                            cols = slice(c * P, (c + 1) * P)
                            half = bank[:, (c % 2) * 2 * P:(c % 2 + 1) * 2 * P]
                            nc.tensor.matmul(half, ones_row[:], vb_row[:], start=True, stop=False)
                            ins = three(half, (xhi[:, cols], xlo[:, cols]),
                                        (uv_hi[:, 2 * P:4 * P], uv_lo[:, 2 * P:4 * P]), first=False)
                        ins.then_inc(s["f_gp"], 1)

                def at_scores(_):
                    pe.wait_ge(s["f_qk"], 2)
                    for b, bank in ((0, psG), (1, psU)):
                        pe.wait_ge(s["f_ga"], 2 + b)
                        for t in range(2):
                            at = b * SEQ + t * P
                            ins = nc.tensor.matmul(bank[:, t * SEQ:(t + 1) * SEQ], at_k[:, at:at + P],
                                                   at_q[:, b * SEQ:(b + 1) * SEQ], start=True, stop=True)
                        ins.then_inc(s["f_sc"], 1)

                def at_mix(_):
                    pe.wait_ge(s["f_ga"], 5)
                    for b in range(2):
                        pe.wait_ge(s["f_sq"], b + 1)
                        for a, bank in ((0, psT), (1, psO)):
                            for t in range(2):
                                ins = nc.tensor.matmul(bank[:, b * SEQ:(b + 1) * SEQ], at_v[:, 2 * b + t, a * P:(a + 1) * P],
                                                       at_s[:, b, t * SEQ:(t + 1) * SEQ], start=t == 0, stop=t == 1)
                            if b:
                                ins.then_inc(s["f_av"], 1)

                def at_out(_):
                    pe.wait_ge(s["f_rl"], 2)
                    for a in range(2):
                        pe.wait_ge(s["f_ua"], a + 1)
                        ins = nc.tensor.matmul(psG, wo[:, a, :], at_ua[:, a, :], start=a == 0, stop=a == 1)
                    ins.then_inc(s["f_go"], 1)
                    pe.wait_ge(s["f_gT"], 1)
                    transposes(psU, lambda c: outT[:, c * P:(c + 1) * P]).then_inc(s["f_gt"], 1)

                run = {"m_norm": m_norm, "m_proj": m_proj, "m_xproj": m_xproj, "m_dt": m_dt, "unit": unit,
                       "m_out": m_out, "f_norm": f_norm, "route": route, "moe": moe, "moe_end": moe_end,
                       "at_proj": at_proj, "at_scores": at_scores, "at_mix": at_mix, "at_out": at_out}
                for step, k in schedule:
                    if step in run:
                        run[step](k)

        def blocks_of(m, e):
            return range(NJ * m + blocks_ready(e - 1), NJ * m + blocks_ready(e)) if e >= 0 else ()

        mamba_in = [("m_ln", 0), ("m_norm", 0), ("m_xt", 0), ("m_proj", 0), ("m_conv", 0), ("m_xproj", 0),
                    ("m_dt", 0), ("m_softplus", 0)]
        units = []
        for n in range(NS):
            if n % NDA == 0:
                units.append(("decays", n // NDA))
            units.append(("unit", n))
        mamba_out = [("m_gate", 0), ("m_out", 0), ("m_res", 0)]
        norm = [[("f_ln", k), ("f_norm", k), ("f_xt", k)] for k in range(3)]
        routing = [[("route", m), ("top2", m)] for m in range(2)]
        experts = [[("moe", m * NE + e) for e in range(NE)] for m in range(2)]
        ends = [[("moe_end", m), ("moe_res", m)] for m in range(2)]
        attention = [("at_proj", 0), ("at_scores", 0), ("at_mix", 0), ("at_out", 0), ("at_res", 0)]

        def merge(a, b):
            out, j = [], 0
            for i, step in enumerate(a):
                out.append(step)
                while j < len(b) and j * len(a) < (i + 1) * len(b):
                    out.append(b[j])
                    j += 1
            return out + b[j:]

        alone = [("setup", 0)] + mamba_in + units[:2] + [("split_weights", 0)] + units[2:] + mamba_out
        rest = (norm[0] + routing[0] + experts[0] + ends[0] + norm[1] + attention + norm[2] + routing[1]
                + experts[1] + ends[1])
        both = merge(norm[0] + routing[0], mamba_in)
        both += merge(experts[0] + ends[0] + norm[1] + attention + norm[2] + routing[1] + experts[1], units + mamba_out)
        both += ends[1]

        numbers = [semaphore.num for semaphore in s.values()]
        sems = range(min(numbers), max(numbers) + 1)

        with ExitStack() as ctx2:
            block_of(alone, 0, None, True)
        nc.all_engine_barrier(sems_to_clear=sems)
        with nc.Fori(1, groups) as g:
            with ExitStack() as ctx2:
                block_of(both, g, g - 1, False)
            nc.all_engine_barrier(sems_to_clear=sems)
        with ExitStack() as ctx2:
            block_of(rest, None, groups - 1, False)


def kernel(**inputs):
    import numpy as np
    import concourse.bacc as bacc
    from concourse.bass_utils import run_bass_kernel_spmd

    w = {k: np.asarray(a) for k, a in inputs.items()}
    a, b, f = "L0_attn_a_", "L0_attn_b_", "L0_ffn_"
    x = w[a + "x"]

    def cols(vector):
        return vector.reshape(-1, P).T

    conv_w = w[a + "conv_w"].reshape(KC, IT, P).transpose(2, 1, 0).reshape(P, IT * KC)
    a_log = w[a + "A_log"].reshape(IT, P, NS).transpose(1, 0, 2).reshape(P, IT * NS)
    uv_b = w[b + "b_uv"]
    vecs = np.concatenate([
        cols(w[a + "norm_scale"]), cols(w[a + "in_b"]), conv_w, cols(w[a + "conv_b"]), cols(w[a + "dt_b"]), a_log,
        cols(w[a + "D"]), cols(w[a + "out_b"]), cols(uv_b[0:2 * P]), cols(uv_b[4 * P:5 * P]),
        w[b + "gamma"].T, w[b + "beta"].T, cols(w[b + "b_out"])], axis=1)
    laid = {
        "x": x.reshape(-1, H),
        "vecs": vecs,
        "in_w": w[a + "in_w"],
        "xproj_w": w[a + "xproj_w"].reshape(IT, P, XP).transpose(1, 0, 2),
        "dt_w": w[a + "dt_w"],
        "out_w": w[a + "out_w"].reshape(IT, P, H).transpose(1, 0, 2),
        "gate_w": w[f + "w_gate"].transpose(1, 0, 2).reshape(H, NE * FI),
        "up_w": w[f + "w_up"].transpose(1, 0, 2).reshape(H, NE * FI),
        "down_w": w[f + "w_down"].reshape(NJ, P, H).transpose(1, 0, 2),
        "uv_w": w[b + "W_uv"],
        "v_b": uv_b[2 * P:4 * P].reshape(1, 2 * P),
        "wo_w": w[b + "W_out"].reshape(2, P, H).transpose(1, 0, 2),
        "router_w": w[f + "router_w"],
    }
    nc = bacc.Bacc("TRN2", target_bir_lowering=False, num_devices=1)
    arrays, args = {}, []
    for name, array in laid.items():
        arrays[name] = np.ascontiguousarray(array)
        args.append(nc.dram_tensor(name, array.shape, mybir.dt.from_np(array.dtype), kind="ExternalInput").ap())
    out = nc.dram_tensor("out", (x.shape[0] * x.shape[1], H), F32, kind="ExternalOutput").ap()
    build(nc, *args, out)
    result = run_bass_kernel_spmd(nc, [arrays], core_ids=[0])
    return result.results[0]["out"].reshape(x.shape)
```

```python
from contextlib import ExitStack

import concourse.bass as bass
from concourse import mybir

ALU = mybir.AluOpType
ACT = mybir.ActivationFunctionType
AX = mybir.AxisListType
F32 = mybir.dt.float32
F32R = mybir.dt.float32r
BF16 = mybir.dt.bfloat16
I32 = mybir.dt.int32
U32 = mybir.dt.uint32

P = 128
H = 128
T = 256
NC = T // P
IT = 2
NS = 16
KC = 4
RK = 64
XP = RK + 2 * NS
NE = 8
FI = 352
NB = -(-FI // P)
FP = NB * P
NP = NE * NB // 2
RING = 6
NDA = 4
NST = 3
EPS = 1e-5
RMS_EPS = 1e-6

V_NS, V_INB, V_CW, V_CB, V_DTB, V_ALOG, V_D, V_OUTB = 0, 1, 5, 13, 15, 17, 49, 51
V_UVB, V_GAMMA, V_BETA, V_WOB, V_END = 52, 55, 57, 59, 60

SEMS = """
 d_vecs d_x d_inw d_xpw d_dtw d_outw d_gate d_up d_down d_uv d_vb d_wo d_rw d_out
 w_zero w_pad w_const w_sel w_A w_half w_inhi w_inlo w_hi w_lo w_iota v_chain a_chain
 m_var m_rstd m_xm m_xt m_hi m_lo m_ph m_eh m_pg m_eg m_g m_conv m_cth m_h m_xp m_xe m_sel m_dt m_z
 m_e m_u m_ln m_delta m_dx m_bc m_dA m_dbx m_scan m_p m_yacc m_y m_yg m_out m_yT m_ot m_x1
 n_var n_rstd n_xm n_xt n_hi n_lo r_lg r_sub r_exp r_w
 f_G f_U f_th f_uc f_a f_in f_dn f_x
 a_pb a_eb a_pu a_eu a_pv a_ev a_b a_qk a_u a_v a_sc a_rl a_sq a_av a_ua a_wo a_woT a_tr a_x
""".split()


def place(plan, start, end, steps):
    for i, step in enumerate(steps):
        plan.append((start + i * (end - start) / len(steps), step))


def mamba_in(p, b):
    return [(name, (p, b)) for name in (
        "m_stats", "m_pow", "m_norm", "m_turn", "m_hi", "m_lo", "m_ph", "m_eh", "m_pg", "m_conv0", "m_eg",
        "m_conv1", "m_g", "m_conv2", "m_conv3", "m_cth", "m_h", "m_xp", "m_xe", "m_dt", "m_s0", "m_z", "m_s1",
        "m_e", "m_u", "m_s2", "m_ln", "m_c", "m_s3", "m_l", "m_delta", "m_dx")]


def place_scan(plan, u, b, need, start, end):
    period = (end - start) / NS
    plan.append((start, ("rows", (u, b, -1, need))))
    for n in range(NS):
        at = start + n * period
        plan.append((start + max(n - 1.6, 0.01 * n) * period, ("decay", (u, b, n, need))))
        plan.append((at + 0.05 * period, ("rows", (u, b, n, need))))
        plan.append((at + 0.1 * period, ("dbx", (u, b, n, need))))
        plan.append((at + 0.45 * period, ("scan", (u, b, n, need))))
        plan.append((at + 0.8 * period, ("mulC", (u, b, n, need))))
        if n:
            plan.append((at + 1.1 * period, ("sum", (u, b, n, need))))


def mamba_out(u, b):
    return [(name, (u, b)) for name in ("m_skip", "m_gate", "m_out", "m_yT", "m_back", "m_res")]


def last_pair(e):
    return (NB * e + NB - 1) // 2


def norm_steps(l, src, dst):
    return [(name, (l, src, dst)) for name in ("n_stats", "n_pow", "n_norm", "n_turn", "n_hi", "n_lo")]


def route_steps(r, w):
    return [(name, (r, w)) for name in ("r_logits", "r_max", "r_exp", "r_prob", "r_top", "r_index", "r_weight")]


def attention_steps(a, b):
    return [(name, (a, b)) for name in (
        "a_pb", "a_eb", "a_pu", "a_b", "a_eu", "a_qk", "a_pv", "a_u", "a_ev", "a_v", "a_sc", "a_rl", "a_sq",
        "a_av", "a_ua", "a_wo", "a_woT", "a_tr", "a_x")]


def place_experts(plan, q, norms, buf, old, new, start, end):
    period = (end - start) / NP
    for j in range(NP):
        at = start + j * period
        for lag, name in ((0.0, "gate"), (0.3, "up"), (0.4, "tanh"), (0.75, "up_copy"), (0.85, "glu"), (1.3, "inner")):
            plan.append((at + lag * period, (name, (q, j, buf, norms))))
    for e in range(NE):
        at = start + last_pair(e) * period
        for lag, name in ((2.1, "down"), (2.7, "weigh")):
            plan.append((at + lag * period, (name, (q, e, buf, old, new))))


def in_order(plan):
    return [step for _, step in sorted(plan, key=lambda entry: entry[0])]


def first_schedule():
    plan = []
    place(plan, 0, 0, [("setup", None)])
    place(plan, 0, 20, mamba_in(0, 0))
    place(plan, 20, 20, [("split_weights", None)])
    place_scan(plan, 0, 0, 1, 20.5, 50)
    place(plan, 21, 48, mamba_in(1, 1))
    place(plan, 50, 54, mamba_out(0, 0))
    place(plan, 47, 47, [("split_up", None)])
    place_scan(plan, 1, 1, 2, 50, 84)
    place(plan, 54, 58, norm_steps(0, "x1_0", 1))
    place(plan, 58, 64, route_steps(0, 1))
    place_experts(plan, 0, 1, 1, "x1_0", "x2_0", 58, 86)
    place(plan, 66, 84, mamba_in(2, 0))
    place(plan, 86, 90, mamba_out(1, 1))
    place(plan, 90, 98, norm_steps(1, "x1_1", 0) + route_steps(1, 0))
    return in_order(plan)


def middle_schedule():
    plan = []
    for q, (norms, buf, old, new) in enumerate(((0, 0, "x1_1", "x2_1"), (2, 1, "x2_0", "x3_0"),
                                                (3, 0, "x1_0", "x2_0"), (5, 1, "x2_1", "x3_1"))):
        place_experts(plan, q, norms, buf, old, new, q * 24.2, (q + 1) * 24.2)
    place_scan(plan, 0, 0, 0, 0, 38)
    place(plan, 2, 38, mamba_in(0, 1))
    place(plan, 39, 43, mamba_out(0, 0))
    place_scan(plan, 1, 1, 1, 43, 85)
    place(plan, 44, 80, mamba_in(1, 0))
    place(plan, 87, 91, mamba_out(1, 1))
    place(plan, 0, 17, norm_steps(0, "x2_0", "A") + attention_steps(0, 0))
    place(plan, 17, 23, norm_steps(1, "x2_0", 1))
    place(plan, 23, 29, route_steps(0, 1))
    place(plan, 43, 47, norm_steps(2, "x1_0", 0))
    place(plan, 47, 53, route_steps(1, 0))
    place(plan, 54, 66, norm_steps(3, "x2_1", "A") + attention_steps(1, 1))
    place(plan, 66, 71, norm_steps(4, "x2_1", 1))
    place(plan, 71, 77, route_steps(2, 1))
    place(plan, 91, 100, norm_steps(5, "x1_1", 0) + route_steps(3, 0))
    return in_order(plan)


def last_schedule():
    plan = []
    for q, (norms, buf, old, new) in enumerate(((0, 0, "x1_1", "x2_1"), (2, 1, "x2_0", "x3_0"),
                                                (4, 0, "x2_1", "x3_1"))):
        place_experts(plan, q, norms, buf, old, new, q * 24, (q + 1) * 24)
    place(plan, 0, 17, norm_steps(0, "x2_0", "A") + attention_steps(0, 0))
    place(plan, 17, 23, norm_steps(1, "x2_0", 1))
    place(plan, 23, 28, route_steps(0, 1))
    place(plan, 28.5, 43, norm_steps(2, "x2_1", "A") + attention_steps(1, 1))
    place(plan, 43, 48, norm_steps(3, "x2_1", 0))
    place(plan, 48, 53, route_steps(1, 0))
    return in_order(plan)


def build(nc, x, vecs, in_w, xproj_w, dt_w, out_w, gate_w, up_w, down_w, uv_w, v_b, wo_w, router_w, out):
    sequences = x.shape[0] // T
    with ExitStack() as ctx:
        def sb(name, shape, dt=F32):
            return ctx.enter_context(nc.sbuf_tensor(name, shape, dt))

        def two(bank):
            return bank.rearrange("p (a t) -> p a t", a=2)

        ps = ctx.enter_context(nc.psum_tensor("ps", [P, 8, 512], F32))
        s = {n: ctx.enter_context(nc.semaphore(n)) for n in SEMS}
        rowps = [two(ps[:, k, :]) for k in range(2)]
        psG, psU, psO = [two(ps[:, 2 + k, :]) for k in range(2)], two(ps[:, 4, :]), ps[:, 5, 0:NC * H]
        chainps, mambaps = ps[:, 6, :], ps[:, 7, :]

        ident = sb("ident", [P, P])
        sel = sb("sel", [96, 2 * NS, P], BF16)
        ones_row = sb("ones_row", [1, P])
        neghalf = sb("neghalf", [P, NC])
        iota_i = sb("iota_i", [P, NE], I32)
        iota8 = sb("iota8", [P, NE])
        vec = sb("vec", [P, V_END])
        half = sb("half", [P, V_END])
        A = sb("A", [P, IT, NS])
        inw_hi = sb("inw_hi", [P, 512], F32R)
        inw_lo = sb("inw_lo", [P, 512], F32R)
        xpw = sb("xpw", [P, IT, XP])
        dtw = sb("dtw", [RK, IT * P])
        outw = sb("outw", [P, IT, H])
        gate_hi = sb("gate_hi", [P, NE * FP], F32R)
        gate_lo = sb("gate_lo", [P, NE * FP], F32R)
        up_hi = sb("up_hi", [P, NE * FP], F32R)
        up_lo = sb("up_lo", [P, NE * FP], F32R)
        down = sb("down", [P, NE, NB, H])
        uv_hi = sb("uv_hi", [P, 640], F32R)
        uv_lo = sb("uv_lo", [P, 640], F32R)
        vb_row = sb("vb_row", [1, 2 * P])
        wo = sb("wo", [P, 2, H])
        rw_raw = sb("rw_raw", [P, NE])
        rw_hi = sb("rw_hi", [P, NE], F32R)
        rw_lo = sb("rw_lo", [P, NE], F32R)

        xin = sb("xin", [P, 2, NC, H])
        m_bn = sb("m_bn", [P, NC, 6])
        m_mv = sb("m_mv", [P, NC, 2])
        m_ve = sb("m_ve", [P, NC])
        m_r = sb("m_r", [P, NC])
        m_xn = sb("m_xn", [P, NC, H])
        m_xhi = sb("m_xhi", [P, T], F32R)
        m_xlo = sb("m_xlo", [P, T], F32R)
        xpad = sb("xpad", [P, IT, T + KC - 1])
        conv = sb("conv", [P, IT, T])
        conv_th = sb("conv_th", [P, IT, T])
        h = sb("h", [P, 2, IT, T])
        gate_z = sb("gate_z", [P, IT, T])
        gate_th = sb("gate_th", [P, IT, T])
        gact = sb("gact", [P, 2, IT, T])
        ts = sb("ts", [RK, T])
        bc_f = sb("bc_f", [96, T])
        bc_r = sb("bc_r", [96, T])
        bc_2 = sb("bc_2", [96, T], BF16)
        bc_3 = sb("bc_3", [96, T], BF16)
        bc_s = sb("bc_s", [96, 2, T], BF16)
        sp_z = sb("sp_z", [P, IT, T])
        sp_e = sb("sp_e", [P, IT, T])
        sp_u = sb("sp_u", [P, IT, T])
        sp_ln = sb("sp_ln", [P, IT, T])
        delta = sb("delta", [P, 2, IT, T])
        dx = sb("dx", [P, 2, IT, T])
        dA = sb("dA", [P, NDA, IT, T])
        dbx_in = sb("dbx_in", [P, 2, IT, T])
        st = sb("st", [P, NST, IT, T])
        yacc = sb("yacc", [P, 2, IT, T])
        yT = sb("yT", [P, T])

        xs = {f"x{k}_{b}": sb(f"x{k}_{b}", [P, NC, H]) for k in (1, 2, 3) for b in (0, 1)}

        n_bn = sb("n_bn", [P, NC, 6])
        n_mv = sb("n_mv", [P, NC, 2])
        n_ve = sb("n_ve", [P, NC])
        n_r = sb("n_r", [P, NC])
        n_xn = sb("n_xn", [P, NC, H])
        xhi = {k: sb(f"xhi_{k}", [P, T], F32R) for k in (0, 1, "A")}
        xlo = {k: sb(f"xlo_{k}", [P, T], F32R) for k in (0, 1, "A")}
        lg_mx = sb("lg_mx", [P, NC])
        lg = sb("lg", [P, NC, NE])
        lg_exp = sb("lg_exp", [P, NC, NE])
        prob = sb("prob", [P, NC, NE])
        total = sb("total", [P, NC])
        total_r = sb("total_r", [P, NC])
        top8 = sb("top8", [P, NC, 8])
        idx8 = sb("idx8", [P, NC, 8], U32)
        idxf = sb("idxf", [P, NC, 2])
        den = sb("den", [P, NC])
        den_r = sb("den_r", [P, NC])
        w2 = sb("w2", [P, NC, 2])
        m1 = sb("m1", [P, NC, NE])
        m2 = sb("m2", [P, NC, NE])
        wts = sb("wts", [P, 2, NC, NE])

        th = sb("th", [P, 2, 2, T])
        uc = sb("uc", [P, 2, 2, T])
        ga = sb("ga", [P, 2, 2, T])
        staging = sb("staging", [P, NE * FP])
        inner = staging[:].rearrange("p (r b t) -> p r b t", r=RING, b=2)
        raw = staging[:].rearrange("p (e f) -> p e f", e=NE)

        at_bz, at_bt, at_base = sb("at_bz", [P, T]), sb("at_bt", [P, T]), sb("at_base", [P, T])
        at_q, at_k = sb("at_q", [P, T]), sb("at_k", [P, T])
        at_uzt = sb("at_uzt", [P, 2, 2, T])
        at_uz, at_ut, at_u = at_uzt[:, 0], at_uzt[:, 1], sb("at_u", [P, 2, T])
        at_v = sb("at_v", [P, NC, 2 * P])
        at_s = sb("at_s", [P, 2, T])
        inw_raw = at_v[:].rearrange("p c e -> p (c e)")
        uv_raw = at_uzt[:].rearrange("p i a t -> p (i a t)")[:, 0:640]
        at_oT = sb("at_oT", [P, T])

        def v(col, n=1):
            return vec[:, col:col + n]

        def hv(col):
            return half[:, col:col + 1]

        def run_schedule(share, schedule):
            for name, arg in schedule:
                if name in share:
                    share[name](arg)

        def block_of(ctx2, schedule, loads, stores, first):
            block = ctx2.enter_context(nc.Block())

            @block.sync
            def _(sp):
                def load(k):
                    row, b, before = loads[k]
                    if before:
                        sp.wait_ge(s["m_x1"], before)
                    rows = x[bass.ds(row * T, T), :]
                    sp.dma_start(xin[:, b], rows.rearrange("(c p) h -> p c h", p=P)).then_inc(s["d_x"], 16)

                if first:
                    sp.dma_start(vec[:], vecs).then_inc(s["d_vecs"], 16)
                    load(0)
                    for sem, dst, src in (("d_inw", inw_raw, in_w), ("d_xpw", xpw[:], xproj_w),
                                          ("d_dtw", dtw[:], dt_w), ("d_outw", outw[:], out_w),
                                          ("d_uv", uv_raw, uv_w), ("d_rw", rw_raw[:], router_w),
                                          ("d_vb", vb_row[:], v_b), ("d_wo", wo[:], wo_w)):
                        sp.dma_start(dst, src).then_inc(s[sem], 16)
                    load(1)
                    experts = "h (e f) -> h e f"
                    sp.dma_start(raw[:, :, 0:FI], gate_w.rearrange(experts, e=NE)).then_inc(s["d_gate"], 16)
                    for k in range(NB):
                        rows = min(P, FI - k * P)
                        sp.dma_start(down[0:rows, :, k, :],
                                     down_w[:, k * P:k * P + rows, :].rearrange("e p h -> p e h")).then_inc(s["d_down"], 16)
                    sp.wait_ge(s["w_lo"], 1)
                    sp.dma_start(raw[:, :, 0:FI], up_w.rearrange(experts, e=NE)).then_inc(s["d_up"], 16)
                    load(2)
                    sp.wait_ge(s["d_vb"], 16)
                    sp.wait_ge(s["d_wo"], 16)
                else:
                    for k in range(len(loads)):
                        load(k)
                for k, (count, row, name) in enumerate(stores):
                    sp.wait_ge(s["f_x"], NE * count)
                    rows = out[bass.ds(row * T, T), :]
                    sp.dma_start(rows.rearrange("(c p) h -> p c h", p=P), xs[name][:]).then_inc(s["d_out"], 16)
                if stores:
                    sp.wait_ge(s["d_out"], 16 * len(stores))

            @block.gpsimd
            def _(pool):
                def setup(_):
                    nc.gpsimd.memset(ident[:], 0.0).then_inc(s["w_zero"], 1)
                    nc.gpsimd.memset(sel[:], 0.0).then_inc(s["w_zero"], 1)
                    nc.gpsimd.memset(raw[:, :, FI:FP], 0.0).then_inc(s["w_pad"], 1)
                    nc.gpsimd.memset(ones_row[:], 1.0)
                    nc.gpsimd.memset(neghalf[:], -0.5)
                    nc.gpsimd.iota(iota_i[:], pattern=[[1, NE]], base=0, channel_multiplier=0).then_inc(s["w_iota"], 1)
                    pool.wait_ge(s["w_zero"], 2)
                    nc.gpsimd.affine_select(out=ident[:], in_=ident[:], compare_op=ALU.not_equal, fill=1.0, base=0,
                                            pattern=[[-1, P]], channel_multiplier=1).then_inc(s["w_const"], 1)
                    pool.wait_ge(s["w_const"], 1)

                def split_weights(_):
                    for q in range(3):
                        if q:
                            pool.wait_ge(s["w_sel"], q)
                        part = sel[32 * q:32 * q + 32, :, :]
                        nc.gpsimd.affine_select(out=part, in_=part, compare_op=ALU.not_equal, fill=1.0, base=0,
                                                pattern=[[-1, 2 * NS], [0, P]],
                                                channel_multiplier=1).then_inc(s["w_sel"], 1)
                    pool.wait_ge(s["w_sel"], 3)
                    for n, (lo, whole, hi) in enumerate(((gate_lo, staging[:], gate_hi), (uv_lo, uv_raw, uv_hi),
                                                       (rw_lo, rw_raw[:], rw_hi))):
                        pool.wait_ge(s["w_hi"], n + 1)
                        nc.gpsimd.tensor_tensor(lo[:], whole, hi[:].bitcast(F32), ALU.subtract).then_inc(s["w_lo"], 1)

                def split_up(_):
                    pool.wait_ge(s["w_hi"], 4)
                    nc.gpsimd.tensor_tensor(up_lo[:], staging[:], up_hi[:].bitcast(F32), ALU.subtract).then_inc(s["w_lo"], 1)

                def m_pow(arg):
                    pool.wait_ge(s["m_var"], arg[0] + 1)
                    nc.gpsimd.tensor_tensor(m_r[:], m_ve[:], neghalf[:], ALU.pow).then_inc(s["m_rstd"], 1)

                def n_pow(arg):
                    pool.wait_ge(s["n_var"], arg[0] + 1)
                    nc.gpsimd.tensor_tensor(n_r[:], n_ve[:], neghalf[:], ALU.pow).then_inc(s["n_rstd"], 1)

                def m_dx(arg):
                    p, b = arg
                    pool.wait_ge(s["m_delta"], p + 1)
                    nc.gpsimd.tensor_tensor(dx[:, b], delta[:, b], h[:, b], ALU.mult).then_inc(s["m_dx"], 1)

                def sum_states(arg):
                    u, b, n, _ = arg
                    i = u * NS + n
                    pool.wait_ge(s["m_p"], i + 1)
                    if n > 1:
                        pool.wait_ge(s["m_yacc"], u * (NS - 1) + n - 1)
                    nc.gpsimd.tensor_tensor(yacc[:, b], st[:, (i - 1) % NST] if n == 1 else yacc[:, b], st[:, i % NST],
                                            ALU.add).then_inc(s["m_yacc"], 1)

                def m_gate(arg):
                    u, b = arg
                    pool.wait_ge(s["m_y"], u + 1)
                    nc.gpsimd.tensor_tensor(yacc[:, b], yacc[:, b], gact[:, b], ALU.mult).then_inc(s["m_yg"], 1)

                def inner_step(arg):
                    q, j, *_ = arg
                    k = q * NP + j
                    pool.wait_ge(s["f_a"], k + 1)
                    pool.wait_ge(s["f_uc"], k + 1)
                    if k >= RING:
                        old_q, old_j = divmod(k - RING, NP)
                        pool.wait_ge(s["f_dn"], old_q * NE + (2 * old_j + 1) // NB + 1)
                    nc.gpsimd.tensor_tensor(inner[:, k % RING], ga[:, k % 2], uc[:, k % 2], ALU.mult).then_inc(s["f_in"], 1)

                def a_sq(arg):
                    pool.wait_ge(s["a_rl"], arg[0] + 1)
                    nc.gpsimd.tensor_tensor(at_s[:], at_s[:], at_s[:], ALU.mult).then_inc(s["a_sq"], 1)

                run_schedule({"setup": setup, "split_weights": split_weights, "split_up": split_up, "m_pow": m_pow, "n_pow": n_pow,
                              "m_dx": m_dx, "sum": sum_states, "m_gate": m_gate, "inner": inner_step, "a_sq": a_sq}, schedule)

            @block.scalar
            def _(act):
                def setup(_):
                    act.wait_ge(s["d_vecs"], 16)
                    nc.scalar.activation(A[:].rearrange("p a n -> p (a n)"), v(V_ALOG, IT * NS), ACT.Exp).then_inc(s["w_A"], 1)
                    act.wait_ge(s["d_inw"], 16)
                    nc.scalar.copy(inw_hi[:], inw_raw).then_inc(s["w_inhi"], 1)
                    act.wait_ge(s["w_half"], 1)

                def split_weights(_):
                    act.wait_ge(s["w_pad"], 1)
                    for sem, whole, hi in (("d_gate", staging[:], gate_hi), ("d_uv", uv_raw, uv_hi),
                                         ("d_rw", rw_raw[:], rw_hi)):
                        act.wait_ge(s[sem], 16)
                        nc.scalar.copy(hi[:], whole).then_inc(s["w_hi"], 1)

                def split_up(_):
                    act.wait_ge(s["d_up"], 16)
                    nc.scalar.copy(up_hi[:], staging[:]).then_inc(s["w_hi"], 1)

                def m_hi(arg):
                    act.wait_ge(s["m_xt"], arg[0] + 1)
                    nc.scalar.activation(m_xhi[:], mambaps[:, 0:T], ACT.Copy, scale=v(V_NS)).then_inc(s["m_hi"], 1)

                def m_eh(arg):
                    act.wait_ge(s["m_ph"], arg[0] + 1)
                    for it in range(IT):
                        ins = nc.scalar.activation(xpad[:, it, KC - 1:], two(mambaps)[:, it], ACT.Identity,
                                                   bias=v(V_INB + it))
                    ins.then_inc(s["m_eh"], 1)

                def m_eg(arg):
                    act.wait_ge(s["m_pg"], arg[0] + 1)
                    for it in range(IT):
                        bias = hv(V_INB + IT + it)
                        nc.scalar.activation(gate_z[:, it], two(mambaps)[:, it], ACT.Identity, bias=bias, scale=0.5)
                        ins = nc.scalar.activation(gate_th[:, it], two(mambaps)[:, it], ACT.Tanh, bias=bias, scale=0.5)
                    ins.then_inc(s["m_eg"], 1)

                def m_cth(arg):
                    act.wait_ge(s["m_conv"], arg[0] + 1)
                    nc.scalar.activation(conv_th[:], conv[:], ACT.Tanh).then_inc(s["m_cth"], 1)

                def m_xe(arg):
                    act.wait_ge(s["m_xp"], arg[0] + 1)
                    nc.scalar.copy(bc_f[64:96, :], mambaps[64:96, 0:T])
                    nc.scalar.copy(ts[:], mambaps[0:RK, 0:T]).then_inc(s["m_xe"], 1)

                def m_z(arg):
                    act.wait_ge(s["m_dt"], arg[0] + 1)
                    for it in range(IT):
                        nc.scalar.activation(sp_e[:, it], two(mambaps)[:, it], ACT.Abs, bias=v(V_DTB + it))
                        ins = nc.scalar.activation(sp_z[:, it], two(mambaps)[:, it], ACT.Identity, bias=v(V_DTB + it))
                    ins.then_inc(s["m_z"], 1)

                def m_e(arg):
                    act.wait_ge(s["m_z"], arg[0] + 1)
                    nc.scalar.activation(sp_e[:], sp_e[:], ACT.Exp, scale=-1.0).then_inc(s["m_e"], 1)

                def m_ln(arg):
                    act.wait_ge(s["m_u"], arg[0] + 1)
                    nc.scalar.activation(sp_ln[:], sp_u[:], ACT.Ln).then_inc(s["m_ln"], 1)

                def decay(arg):
                    u, b, n, need = arg
                    i = u * NS + n
                    if need:
                        act.wait_ge(s["m_delta"], need)
                    if i >= NDA:
                        act.wait_ge(s["m_scan"], i - NDA + 1)
                    for it in range(IT):
                        ins = nc.scalar.activation(dA[:, i % NDA, it, 1:], delta[:, b, it, 1:], ACT.Exp,
                                                   scale=A[:, it, n:n + 1])
                    ins.then_inc(s["m_dA"], 1)

                def m_yT(arg):
                    act.wait_ge(s["m_out"], arg[0] + 1)
                    nc.scalar.activation(yT[:], mambaps[:, 0:T], ACT.Identity, bias=v(V_OUTB)).then_inc(s["m_yT"], 1)

                def n_hi(arg):
                    l, _, dst = arg
                    act.wait_ge(s["n_xt"], l + 1)
                    nc.scalar.copy(xhi[dst][:], chainps[:, 0:T]).then_inc(s["n_hi"], 1)

                def r_exp(arg):
                    act.wait_ge(s["r_sub"], arg[0] + 1)
                    nc.scalar.activation(lg_exp[:], lg[:], ACT.Exp).then_inc(s["r_exp"], 1)

                def tanh(arg):
                    q, j, *_ = arg
                    k = q * NP + j
                    act.wait_ge(s["f_G"], k + 1)
                    if k >= 2:
                        act.wait_ge(s["f_a"], k - 1)
                    nc.scalar.activation(th[:, k % 2], psG[k % 2], ACT.Tanh, scale=0.5).then_inc(s["f_th"], 1)

                def up_copy(arg):
                    q, j, *_ = arg
                    k = q * NP + j
                    act.wait_ge(s["f_U"], k + 1)
                    if k >= 2:
                        act.wait_ge(s["f_in"], k - 1)
                    nc.scalar.copy(uc[:, k % 2], psU).then_inc(s["f_uc"], 1)

                def a_eb(arg):
                    act.wait_ge(s["a_pb"], arg[0] + 1)
                    bias = hv(V_UVB + 2)
                    nc.scalar.activation(at_bz[:], chainps[:, 0:T], ACT.Identity, bias=bias, scale=0.5)
                    nc.scalar.activation(at_bt[:], chainps[:, 0:T], ACT.Tanh, bias=bias, scale=0.5).then_inc(s["a_eb"], 1)

                def a_eu(arg):
                    act.wait_ge(s["a_pu"], arg[0] + 1)
                    for a in range(2):
                        bias = hv(V_UVB + a)
                        nc.scalar.activation(at_uz[:, a], two(chainps)[:, a], ACT.Identity, bias=bias, scale=0.5)
                        ins = nc.scalar.activation(at_ut[:, a], two(chainps)[:, a], ACT.Tanh, bias=bias, scale=0.5)
                    ins.then_inc(s["a_eu"], 1)

                def a_ev(arg):
                    act.wait_ge(s["a_pv"], arg[0] + 1)
                    nc.scalar.activation(at_v[:], two(chainps), ACT.Tanh, scale=0.5).then_inc(s["a_ev"], 1)

                def a_rl(arg):
                    act.wait_ge(s["a_sc"], arg[0] + 1)
                    nc.scalar.activation(at_s[:], two(chainps), ACT.Relu, scale=1.0 / T).then_inc(s["a_rl"], 1)

                def a_woT(arg):
                    act.wait_ge(s["a_wo"], arg[0] + 1)
                    nc.scalar.activation(at_oT[:], chainps[:, 0:T], ACT.Identity, bias=v(V_WOB)).then_inc(s["a_woT"], 1)

                run_schedule({"setup": setup, "split_weights": split_weights, "split_up": split_up, "m_hi": m_hi,
                              "m_eh": m_eh, "m_eg": m_eg, "m_cth": m_cth, "m_xe": m_xe, "m_z": m_z, "m_e": m_e,
                              "m_ln": m_ln, "decay": decay, "m_yT": m_yT, "n_hi": n_hi, "r_exp": r_exp, "tanh": tanh,
                              "up_copy": up_copy, "a_eb": a_eb, "a_eu": a_eu, "a_ev": a_ev, "a_rl": a_rl,
                              "a_woT": a_woT}, schedule)

            @block.vector
            def _(dve):
                chain = [0]

                def mark(ins):
                    chain[0] += 1
                    ins.then_inc(s["v_chain"], 1)
                    return chain[0]

                def link():
                    dve.wait_ge(s["v_chain"], chain[0])

                def setup(_):
                    mark(nc.vector.memset(xpad[:, :, 0:KC - 1], 0.0))
                    mark(nc.vector.memset(dA[:, :, :, 0:1].rearrange("p n a o -> p (n a) o"), 0.0))
                    dve.wait_ge(s["w_iota"], 1)
                    mark(nc.vector.tensor_copy(iota8[:], iota_i[:]))
                    dve.wait_ge(s["d_vecs"], 16)
                    nc.vector.tensor_scalar(half[:], vec[:], 0.5, None, ALU.mult).then_inc(s["w_half"], 1)
                    dve.wait_ge(s["w_A"], 1)
                    a = A[:].rearrange("p a n -> p (a n)")
                    nc.vector.tensor_scalar(a, a, -1.0, None, ALU.mult).then_inc(s["w_A"], 1)
                    dve.wait_ge(s["w_inhi"], 1)
                    nc.vector.tensor_tensor(inw_lo[:], inw_raw, inw_hi[:].bitcast(F32), ALU.subtract).then_inc(s["w_inlo"], 1)

                def norm_stats(xt, bn, mv):
                    for c in range(NC):
                        mark(nc.vector.bn_stats(bn[:, c, :], xt[:, c, :]))
                    link()
                    for c in range(NC):
                        mark(nc.vector.bn_aggr(mv[:, c, :], bn[:, c, :]))
                    link()

                def m_stats(arg):
                    p, b = arg
                    dve.wait_ge(s["d_x"], 16 * (p + 1))
                    norm_stats(xin[:, b], m_bn, m_mv)
                    nc.vector.tensor_scalar(m_ve[:], m_mv[:, :, 1], 1.0 + RMS_EPS, RMS_EPS * EPS,
                                            ALU.mult, ALU.add).then_inc(s["m_var"], 1)

                def m_norm(arg):
                    p, b = arg
                    dve.wait_ge(s["m_rstd"], p + 1)
                    for c in range(NC):
                        ins = nc.vector.tensor_scalar(m_xn[:, c, :], xin[:, b, c, :], m_mv[:, c, 0:1], m_r[:, c:c + 1],
                                                      ALU.subtract, ALU.mult)
                    ins.then_inc(s["m_xm"], 1)

                def m_lo(arg):
                    dve.wait_ge(s["m_hi"], arg[0] + 1)
                    nc.vector.scalar_tensor_tensor(out=m_xlo[:], in0=mambaps[:, 0:T], scalar=v(V_NS),
                                                   in1=m_xhi[:].bitcast(F32), op0=ALU.mult,
                                                   op1=ALU.subtract).then_inc(s["m_lo"], 1)

                conv_mark = [0]

                def conv_tap(k):
                    def tap(arg):
                        if k == 0:
                            dve.wait_ge(s["m_eh"], arg[0] + 1)
                        else:
                            dve.wait_ge(s["v_chain"], conv_mark[0])
                        for it in range(IT):
                            w, src, dst = hv(V_CW + it * KC + k), xpad[:, it, k:k + T], conv[:, it]
                            if k == 0:
                                ins = nc.vector.tensor_scalar(dst, src, w, hv(V_CB + it), ALU.mult, ALU.add)
                            else:
                                ins = nc.vector.scalar_tensor_tensor(out=dst, in0=src, scalar=w, in1=dst,
                                                                     op0=ALU.mult, op1=ALU.add)
                            if k < KC - 1:
                                conv_mark[0] = mark(ins)
                        if k == KC - 1:
                            ins.then_inc(s["m_conv"], 1)
                    return tap

                def m_g(arg):
                    p, b = arg
                    dve.wait_ge(s["m_eg"], p + 1)
                    nc.vector.scalar_tensor_tensor(out=gact[:, b], in0=gate_th[:], scalar=1.0, in1=gate_z[:],
                                                   op0=ALU.add, op1=ALU.mult).then_inc(s["m_g"], 1)

                def m_h(arg):
                    p, b = arg
                    dve.wait_ge(s["m_cth"], p + 1)
                    nc.vector.scalar_tensor_tensor(out=h[:, b], in0=conv_th[:], scalar=1.0, in1=conv[:],
                                                   op0=ALU.add, op1=ALU.mult).then_inc(s["m_h"], 1)

                split_mark = [0]

                def m_s0(arg):
                    p, b = arg
                    dve.wait_ge(s["m_xe"], p + 1)
                    split_mark[0] = mark(nc.vector.tensor_copy(bc_s[64:96, b], bc_f[64:96, :]))

                def m_s1(arg):
                    dve.wait_ge(s["v_chain"], split_mark[0])
                    split_mark[0] = mark(nc.vector.tensor_tensor(bc_r[64:96, :], bc_f[64:96, :], bc_s[64:96, arg[1]],
                                                                 ALU.subtract))

                def m_s2(arg):
                    dve.wait_ge(s["v_chain"], split_mark[0])
                    split_mark[0] = mark(nc.vector.tensor_copy(bc_2[64:96, :], bc_r[64:96, :]))

                def m_s3(arg):
                    b = arg[1]
                    dve.wait_ge(s["v_chain"], split_mark[0])
                    mark(nc.vector.tensor_tensor(bc_3[64:96, :], bc_r[64:96, :], bc_2[64:96, :], ALU.subtract))
                    mark(nc.vector.tensor_copy(bc_s[32:64, b], bc_2[64:96, :]))
                    link()
                    nc.vector.tensor_copy(bc_s[0:32, b], bc_3[64:96, :]).then_inc(s["m_sel"], 1)

                sp_mark = [0]

                def m_u(arg):
                    dve.wait_ge(s["m_e"], arg[0] + 1)
                    nc.vector.tensor_scalar(sp_u[:], sp_e[:], 1.0, None, ALU.add).then_inc(s["m_u"], 1)

                def m_c(arg):
                    dve.wait_ge(s["m_u"], arg[0] + 1)
                    sp_mark[0] = mark(nc.vector.scalar_tensor_tensor(out=sp_e[:], in0=sp_u[:], scalar=-1.0, in1=sp_e[:],
                                                                     op0=ALU.add, op1=ALU.subtract))

                def m_l(arg):
                    dve.wait_ge(s["v_chain"], sp_mark[0])
                    dve.wait_ge(s["m_ln"], arg[0] + 1)
                    sp_mark[0] = mark(nc.vector.tensor_tensor(sp_e[:], sp_ln[:], sp_e[:], ALU.subtract))

                def m_delta(arg):
                    dve.wait_ge(s["v_chain"], sp_mark[0])
                    nc.vector.scalar_tensor_tensor(out=delta[:, arg[1]], in0=sp_z[:], scalar=0.0, in1=sp_e[:],
                                                   op0=ALU.max, op1=ALU.add).then_inc(s["m_delta"], 1)

                def dbx(arg):
                    u, b, n, need = arg
                    i = u * NS + n
                    if need:
                        dve.wait_ge(s["m_dx"], need)
                    r = u * (NS + 1) + n
                    dve.wait_ge(s["m_bc"], r + 1)
                    if i > 1:
                        dve.wait_ge(s["m_scan"], i - 1)
                    nc.vector.tensor_tensor(dbx_in[:, i % 2], dx[:, b], rowps[r % 2][:, 0:1].broadcast_to([P, IT, T]),
                                            ALU.mult).then_inc(s["m_dbx"], 1)

                def scan(arg):
                    u, b, n, _ = arg
                    i = u * NS + n
                    dve.wait_ge(s["m_dA"], i + 1)
                    dve.wait_ge(s["m_dbx"], i + 1)
                    if i >= NST:
                        old_u, old_n = divmod(i - NST, NS)
                        dve.wait_ge(s["m_yacc"], old_u * (NS - 1) + max(1, old_n))
                    nc.vector.tensor_tensor_scan(out=st[:, i % NST].rearrange("p a t -> p (a t)"),
                                                 data0=dA[:, i % NDA].rearrange("p a t -> p (a t)"),
                                                 data1=dbx_in[:, i % 2].rearrange("p a t -> p (a t)"), initial=0.0,
                                                 op0=ALU.mult, op1=ALU.add).then_inc(s["m_scan"], 1)

                def mulC(arg):
                    u, b, n, _ = arg
                    i = u * NS + n
                    r = u * (NS + 1) + n + 1
                    dve.wait_ge(s["m_bc"], r + 1)
                    dve.wait_ge(s["m_scan"], i + 1)
                    nc.vector.tensor_tensor(st[:, i % NST], st[:, i % NST], rowps[r % 2][:, 1:2].broadcast_to([P, IT, T]),
                                            ALU.mult).then_inc(s["m_p"], 1)

                def m_skip(arg):
                    u, b = arg
                    dve.wait_ge(s["m_yacc"], (u + 1) * (NS - 1))
                    for it in range(IT):
                        ins = nc.vector.scalar_tensor_tensor(out=yacc[:, b, it], in0=h[:, b, it], scalar=v(V_D + it),
                                                             in1=yacc[:, b, it], op0=ALU.mult, op1=ALU.add)
                    ins.then_inc(s["m_y"], 1)

                def m_res(arg):
                    u, b = arg
                    dve.wait_ge(s["m_ot"], u + 1)
                    nc.vector.tensor_tensor(xs[f"x1_{b}"][:], xin[:, b], two(mambaps[:, T:2 * T]), ALU.add).then_inc(s["m_x1"], 1)
                    dve.wait_ge(s["m_x1"], u + 1)

                def n_stats(arg):
                    l, src, _ = arg
                    link()
                    norm_stats(xs[src], n_bn, n_mv)
                    nc.vector.tensor_scalar(n_ve[:], n_mv[:, :, 1], EPS, None, ALU.add).then_inc(s["n_var"], 1)

                def n_norm(arg):
                    l, src, _ = arg
                    dve.wait_ge(s["n_rstd"], l + 1)
                    for c in range(NC):
                        ins = nc.vector.tensor_scalar(n_xn[:, c, :], xs[src][:, c, :], n_mv[:, c, 0:1], n_r[:, c:c + 1],
                                                      ALU.subtract, ALU.mult)
                    ins.then_inc(s["n_xm"], 1)

                def n_lo(arg):
                    l, _, dst = arg
                    dve.wait_ge(s["n_hi"], l + 1)
                    nc.vector.tensor_tensor(xlo[dst][:], chainps[:, 0:T], xhi[dst][:].bitcast(F32),
                                            ALU.subtract).then_inc(s["n_lo"], 1)

                def wide(a, n):
                    return a[:].unsqueeze(2).broadcast_to([P, NC, n])

                def r_max(arg):
                    dve.wait_ge(s["r_lg"], arg[0] + 1)
                    logits = chainps[:, T:T + NC * NE].rearrange("p (c e) -> p c e", c=NC)
                    mark(nc.vector.reduce_max(lg_mx[:], logits, AX.X))
                    link()
                    nc.vector.tensor_tensor(lg[:], logits, wide(lg_mx, NE), ALU.subtract).then_inc(s["r_sub"], 1)

                def r_prob(arg):
                    dve.wait_ge(s["r_exp"], arg[0] + 1)
                    mark(nc.vector.tensor_reduce(total[:], lg_exp[:], AX.X, ALU.add))
                    link()
                    mark(nc.vector.reciprocal(total_r[:], total[:]))
                    link()
                    mark(nc.vector.tensor_tensor(prob[:], lg_exp[:], wide(total_r, NE), ALU.mult))

                def r_top(arg):
                    link()
                    for c in range(NC):
                        mark(nc.vector.max(top8[:, c, :], prob[:, c, :]))

                def r_index(arg):
                    link()
                    for c in range(NC):
                        mark(nc.vector.max_index(idx8[:, c, :], top8[:, c, :], prob[:, c, :]))
                    mark(nc.vector.tensor_tensor(den[:], top8[:, :, 0], top8[:, :, 1], ALU.add))
                    link()
                    mark(nc.vector.tensor_copy(idxf[:], idx8[:, :, 0:2]))
                    mark(nc.vector.reciprocal(den_r[:], den[:]))

                def r_weight(arg):
                    _, w = arg
                    link()
                    mark(nc.vector.scalar_tensor_tensor(out=w2[:], in0=top8[:, :, 0:2], scalar=0.5, in1=wide(den_r, 2),
                                                        op0=ALU.mult, op1=ALU.mult))
                    link()
                    for c in range(NC):
                        for j, mk in ((0, m1), (1, m2)):
                            mark(nc.vector.tensor_scalar(mk[:, c, :], iota8[:], idxf[:, c, j:j + 1], w2[:, c, j:j + 1],
                                                         ALU.is_equal, ALU.mult))
                    link()
                    nc.vector.tensor_tensor(wts[:, w], m1[:], m2[:], ALU.add).then_inc(s["r_w"], 1)

                def glu(arg):
                    q, j, *_ = arg
                    k = q * NP + j
                    dve.wait_ge(s["f_th"], k + 1)
                    if k >= 2:
                        dve.wait_ge(s["f_in"], k - 1)
                    nc.vector.scalar_tensor_tensor(out=ga[:, k % 2], in0=th[:, k % 2], scalar=1.0, in1=psG[k % 2],
                                                   op0=ALU.add, op1=ALU.mult).then_inc(s["f_a"], 1)

                def weigh(arg):
                    q, e, buf, old, new = arg
                    k = q * NE + e
                    dve.wait_ge(s["f_dn"], k + 1)
                    if e == 0 and q + first:
                        dve.wait_ge(s["r_w"], q + first)
                    if e:
                        dve.wait_ge(s["f_x"], k)
                    for c in range(NC):
                        before = xs[new if e else old][:, c, :]
                        ins = nc.vector.scalar_tensor_tensor(out=xs[new][:, c, :], in0=psO[:, c * H:(c + 1) * H],
                                                             scalar=wts[:, buf, c, e:e + 1], in1=before, op0=ALU.mult,
                                                             op1=ALU.add)
                    ins.then_inc(s["f_x"], 1)
                    if e == NE - 1:
                        dve.wait_ge(s["f_x"], k + 1)

                def silu2(dst, t, z, sem):
                    nc.vector.scalar_tensor_tensor(out=dst, in0=t, scalar=1.0, in1=z, op0=ALU.add,
                                                   op1=ALU.mult).then_inc(s[sem], 1)

                def a_b(arg):
                    dve.wait_ge(s["a_eb"], arg[0] + 1)
                    silu2(at_base[:], at_bt[:], at_bz[:], "a_b")

                def a_qk(arg):
                    dve.wait_ge(s["a_b"], arg[0] + 1)
                    for j, dst in ((0, at_q), (1, at_k)):
                        ins = nc.vector.tensor_scalar(dst[:], at_base[:], v(V_GAMMA + j), v(V_BETA + j), ALU.mult, ALU.add)
                    ins.then_inc(s["a_qk"], 1)

                def a_u(arg):
                    dve.wait_ge(s["a_eu"], arg[0] + 1)
                    silu2(at_u[:], at_ut, at_uz, "a_u")

                def a_v(arg):
                    dve.wait_ge(s["a_ev"], arg[0] + 1)
                    silu2(at_v[:], at_v[:], two(chainps), "a_v")

                def a_ua(arg):
                    dve.wait_ge(s["a_av"], arg[0] + 1)
                    dve.wait_ge(s["a_u"], arg[0] + 1)
                    nc.vector.scalar_tensor_tensor(out=at_u[:], in0=at_u[:], scalar=0.5, in1=two(chainps),
                                                   op0=ALU.mult, op1=ALU.mult).then_inc(s["a_ua"], 1)

                def a_x(arg):
                    a, b = arg
                    dve.wait_ge(s["a_tr"], a + 1)
                    name = f"x2_{b}"
                    nc.vector.tensor_tensor(xs[name][:], xs[name][:], two(chainps[:, T:2 * T]), ALU.add).then_inc(s["a_x"], 1)
                    dve.wait_ge(s["a_x"], a + 1)

                run_schedule({"setup": setup, "m_stats": m_stats, "m_norm": m_norm, "m_lo": m_lo, "m_conv0": conv_tap(0),
                              "m_conv1": conv_tap(1), "m_conv2": conv_tap(2), "m_conv3": conv_tap(3), "m_g": m_g,
                              "m_h": m_h, "m_s0": m_s0, "m_s1": m_s1, "m_s2": m_s2, "m_s3": m_s3, "m_u": m_u, "m_c": m_c,
                              "m_l": m_l, "m_delta": m_delta, "dbx": dbx, "scan": scan, "mulC": mulC, "m_skip": m_skip,
                              "m_res": m_res, "n_stats": n_stats, "n_norm": n_norm, "n_lo": n_lo, "r_max": r_max,
                              "r_prob": r_prob, "r_top": r_top, "r_index": r_index, "r_weight": r_weight, "glu": glu,
                              "weigh": weigh, "a_b": a_b, "a_qk": a_qk, "a_u": a_u, "a_v": a_v, "a_ua": a_ua,
                              "a_x": a_x}, schedule)

            @block.tensor
            def _(pe):
                reader = {"chain": None, "mamba": None}

                def free(bank):
                    if reader[bank]:
                        sem, value = reader[bank]
                        pe.wait_ge(s[sem], value)

                def transposes(bank, src):
                    for c in range(NC):
                        ins = nc.tensor.transpose(bank[:, c * P:(c + 1) * P], src[:, c * P:(c + 1) * P], ident[:])
                    return ins

                def three(bank, w, xv, start=True):
                    nc.tensor.matmul(bank, w[0], xv[0], start=start, stop=False)
                    nc.tensor.matmul(bank, w[0], xv[1], start=False, stop=False)
                    return nc.tensor.matmul(bank, w[1], xv[0], start=False, stop=True)

                def m_turn(arg):
                    p, b = arg
                    if first:
                        pe.wait_ge(s["w_const"], 1)
                    free("mamba")
                    pe.wait_ge(s["m_xm"], p + 1)
                    transposes(mambaps, m_xn[:].rearrange("p c h -> p (c h)")).then_inc(s["m_xt"], 1)
                    reader["mamba"] = ("m_lo", p + 1)

                def project(p, first_tile, sem):
                    free("mamba")
                    for it in range(IT):
                        cols = slice((first_tile + it) * P, (first_tile + it + 1) * P)
                        ins = three(two(mambaps)[:, it], (inw_hi[:, cols], inw_lo[:, cols]), (m_xhi[:], m_xlo[:]))
                    ins.then_inc(s[sem], 1)

                def m_ph(arg):
                    if first:
                        pe.wait_ge(s["w_inlo"], 1)
                    project(arg[0], 0, "m_ph")
                    reader["mamba"] = ("m_eh", arg[0] + 1)

                def m_pg(arg):
                    project(arg[0], IT, "m_pg")
                    reader["mamba"] = ("m_eg", arg[0] + 1)

                def m_xp(arg):
                    p, b = arg
                    if first:
                        pe.wait_ge(s["d_xpw"], 16)
                    free("mamba")
                    pe.wait_ge(s["m_h"], p + 1)
                    for it in range(IT):
                        ins = nc.tensor.matmul(mambaps[0:XP, 0:T], xpw[:, it, :], h[:, b, it], start=it == 0,
                                               stop=it == IT - 1)
                    ins.then_inc(s["m_xp"], 1)
                    reader["mamba"] = ("m_xe", p + 1)

                def m_dt(arg):
                    p, b = arg
                    if first:
                        pe.wait_ge(s["d_dtw"], 16)
                    free("mamba")
                    for it in range(IT):
                        ins = nc.tensor.matmul(two(mambaps)[:, it], dtw[:, it * P:(it + 1) * P], ts[:], start=True, stop=True)
                    ins.then_inc(s["m_dt"], 1)
                    reader["mamba"] = ("m_z", p + 1)

                def rows(arg):
                    u, b, n, need = arg
                    r = u * (NS + 1) + n + 1
                    if first and r == 0:
                        pe.wait_ge(s["w_sel"], 3)
                    if need and n < 0:
                        pe.wait_ge(s["m_sel"], need)
                    used_b = u * NS + max(n, 0)
                    used_c = u * NS + (max(n - 1, 0) if n >= 0 else -1)
                    if used_b:
                        pe.wait_ge(s["m_dbx"], used_b)
                    if used_c > 0:
                        pe.wait_ge(s["m_p"], used_c)
                    if n >= 0:
                        ins = nc.tensor.matmul(rowps[r % 2][:, 1], sel[:, NS + n, :], bc_s[:, b], start=True, stop=True)
                    if n + 1 < NS:
                        ins = nc.tensor.matmul(rowps[r % 2][:, 0], sel[:, n + 1, :], bc_s[:, b], start=True, stop=True)
                    ins.then_inc(s["m_bc"], 1)

                def m_out(arg):
                    u, b = arg
                    if first:
                        pe.wait_ge(s["d_outw"], 16)
                    free("mamba")
                    pe.wait_ge(s["m_yg"], u + 1)
                    for it in range(IT):
                        ins = nc.tensor.matmul(mambaps[:, 0:T], outw[:, it, :], yacc[:, b, it], start=it == 0,
                                               stop=it == IT - 1)
                    ins.then_inc(s["m_out"], 1)

                def m_back(arg):
                    u, _ = arg
                    pe.wait_ge(s["m_yT"], u + 1)
                    transposes(mambaps[:, T:2 * T], yT).then_inc(s["m_ot"], 1)
                    reader["mamba"] = ("m_x1", u + 1)

                def n_turn(arg):
                    l = arg[0]
                    free("chain")
                    pe.wait_ge(s["n_xm"], l + 1)
                    transposes(chainps, n_xn[:].rearrange("p c h -> p (c h)")).then_inc(s["n_xt"], 1)
                    reader["chain"] = ("n_lo", l + 1)

                def r_logits(arg):
                    r, w = arg
                    if first:
                        pe.wait_ge(s["w_lo"], 3)
                    free("chain")
                    for c in range(NC):
                        cols = slice(c * P, (c + 1) * P)
                        ins = three(chainps[:, T + c * NE:T + (c + 1) * NE], (xhi[w][:, cols], xlo[w][:, cols]),
                                    (rw_hi[:], rw_lo[:]))
                    ins.then_inc(s["r_lg"], 1)
                    reader["chain"] = ("r_sub", r + 1)

                def products(bank, w, q, j, buf):
                    for k in range(2):
                        cols = slice((2 * j + k) * P, (2 * j + k + 1) * P)
                        ins = three(bank[:, k], (w[0][:, cols], w[1][:, cols]), (xhi[buf][:], xlo[buf][:]))
                    return ins

                def gate(arg):
                    q, j, buf, norms = arg
                    k = q * NP + j
                    if k >= 2:
                        pe.wait_ge(s["f_a"], k - 1)
                    if first and k == 0:
                        pe.wait_ge(s["w_lo"], 3)
                    if j == 0 and norms:
                        pe.wait_ge(s["n_lo"], norms)
                    products(psG[k % 2], (gate_hi, gate_lo), q, j, buf).then_inc(s["f_G"], 1)

                def up(arg):
                    q, j, buf, norms = arg
                    k = q * NP + j
                    if k:
                        pe.wait_ge(s["f_uc"], k)
                    elif first:
                        pe.wait_ge(s["w_lo"], 4)
                    products(psU, (up_hi, up_lo), q, j, buf).then_inc(s["f_U"], 1)

                def lower(arg):
                    q, e, *_ = arg
                    k = q * NE + e
                    if first and k == 0:
                        pe.wait_ge(s["d_down"], 16 * NB)
                    pe.wait_ge(s["f_in"], q * NP + last_pair(e) + 1)
                    if k:
                        pe.wait_ge(s["f_x"], k)
                    for c in range(NC):
                        for n in range(NB):
                            rows = min(P, FI - n * P)
                            pair, half_pair = divmod(NB * e + n, 2)
                            act_in = inner[0:rows, (q * NP + pair) % RING, half_pair, c * P:(c + 1) * P]
                            ins = nc.tensor.matmul(psO[:, c * H:(c + 1) * H], act_in, down[0:rows, e, n, :],
                                                   start=n == 0, stop=n == NB - 1)
                    ins.then_inc(s["f_dn"], 1)

                xa = (xhi["A"], xlo["A"])

                def a_pb(arg):
                    free("chain")
                    three(chainps[:, 0:T], (uv_hi[:, 4 * P:5 * P], uv_lo[:, 4 * P:5 * P]),
                          (xa[0][:], xa[1][:])).then_inc(s["a_pb"], 1)
                    reader["chain"] = ("a_eb", arg[0] + 1)

                def a_pu(arg):
                    free("chain")
                    for a in range(2):
                        cols = slice(a * P, (a + 1) * P)
                        ins = three(two(chainps)[:, a], (uv_hi[:, cols], uv_lo[:, cols]), (xa[0][:], xa[1][:]))
                    ins.then_inc(s["a_pu"], 1)
                    reader["chain"] = ("a_eu", arg[0] + 1)

                def a_pv(arg):
                    free("chain")
                    for c in range(NC):
                        cols = slice(c * P, (c + 1) * P)
                        bank = two(chainps)[:, c]
                        nc.tensor.matmul(bank, ones_row[:], vb_row[:], start=True, stop=False)
                        ins = three(bank, (xa[0][:, cols], xa[1][:, cols]),
                                    (uv_hi[:, 2 * P:4 * P], uv_lo[:, 2 * P:4 * P]), start=False)
                    ins.then_inc(s["a_pv"], 1)
                    reader["chain"] = ("a_v", arg[0] + 1)

                def a_sc(arg):
                    free("chain")
                    pe.wait_ge(s["a_qk"], arg[0] + 1)
                    for c in range(NC):
                        ins = nc.tensor.matmul(two(chainps)[:, c], at_k[:, c * P:(c + 1) * P], at_q[:], start=True, stop=True)
                    ins.then_inc(s["a_sc"], 1)
                    reader["chain"] = ("a_rl", arg[0] + 1)

                def a_av(arg):
                    free("chain")
                    pe.wait_ge(s["a_sq"], arg[0] + 1)
                    for a in range(2):
                        for c in range(NC):
                            ins = nc.tensor.matmul(two(chainps)[:, a], at_v[:, c, a * P:(a + 1) * P], at_s[:, c],
                                                   start=c == 0, stop=c == NC - 1)
                    ins.then_inc(s["a_av"], 1)
                    reader["chain"] = ("a_ua", arg[0] + 1)

                def a_wo(arg):
                    free("chain")
                    for a in range(2):
                        ins = nc.tensor.matmul(chainps[:, 0:T], wo[:, a, :], at_u[:, a], start=a == 0, stop=a == 1)
                    ins.then_inc(s["a_wo"], 1)

                def a_tr(arg):
                    pe.wait_ge(s["a_woT"], arg[0] + 1)
                    transposes(chainps[:, T:2 * T], at_oT).then_inc(s["a_tr"], 1)
                    reader["chain"] = ("a_x", arg[0] + 1)

                run_schedule({"m_turn": m_turn, "m_ph": m_ph, "m_pg": m_pg, "m_xp": m_xp, "m_dt": m_dt, "rows": rows,
                              "m_out": m_out, "m_back": m_back, "n_turn": n_turn, "r_logits": r_logits,
                              "gate": gate, "up": up, "down": lower, "a_pb": a_pb, "a_pu": a_pu,
                              "a_pv": a_pv, "a_sc": a_sc, "a_av": a_av, "a_wo": a_wo, "a_tr": a_tr}, schedule)

        numbers = [semaphore.num for semaphore in s.values()]
        sems = range(min(numbers), max(numbers) + 1)

        with ExitStack() as ctx2:
            block_of(ctx2, first_schedule(), [(0, 0, 0), (1, 1, 0), (2, 0, 1)], [], True)
        nc.all_engine_barrier(sems_to_clear=sems)
        with nc.Fori(1, sequences // 2) as g:
            with ExitStack() as ctx2:
                block_of(ctx2, middle_schedule(), [(2 * g + 1, 1, 0), ((2 * g + 2) % sequences, 0, 1)],
                         [(2, 2 * g - 2, "x3_0"), (4, 2 * g - 1, "x3_1")], False)
            nc.all_engine_barrier(sems_to_clear=sems)
        with ExitStack() as ctx2:
            block_of(ctx2, last_schedule(), [], [(2, sequences - 2, "x3_0"), (3, sequences - 1, "x3_1")], False)


def kernel(**inputs):
    import numpy as np
    import concourse.bacc as bacc
    from concourse.bass_utils import run_bass_kernel_spmd

    w = {k: np.asarray(a) for k, a in inputs.items()}
    a, b, f = "L0_attn_a_", "L0_attn_b_", "L0_ffn_"
    x = w[a + "x"]

    def cols(vector):
        return vector.reshape(-1, P).T

    conv_w = w[a + "conv_w"].reshape(KC, IT, P).transpose(2, 1, 0).reshape(P, IT * KC)
    a_log = w[a + "A_log"].reshape(IT, P, NS).transpose(1, 0, 2).reshape(P, IT * NS)
    uv_b = w[b + "b_uv"]
    vecs = np.concatenate([
        cols(w[a + "norm_scale"]), cols(w[a + "in_b"]), conv_w, cols(w[a + "conv_b"]), cols(w[a + "dt_b"]), a_log,
        cols(w[a + "D"]), cols(w[a + "out_b"]), cols(uv_b[0:2 * P]), cols(uv_b[4 * P:5 * P]),
        w[b + "gamma"].T, w[b + "beta"].T, cols(w[b + "b_out"])], axis=1)
    laid = {
        "x": x.reshape(-1, H),
        "vecs": vecs,
        "in_w": w[a + "in_w"],
        "xproj_w": w[a + "xproj_w"].reshape(IT, P, XP).transpose(1, 0, 2),
        "dt_w": w[a + "dt_w"],
        "out_w": w[a + "out_w"].reshape(IT, P, H).transpose(1, 0, 2),
        "gate_w": w[f + "w_gate"].transpose(1, 0, 2).reshape(H, NE * FI),
        "up_w": w[f + "w_up"].transpose(1, 0, 2).reshape(H, NE * FI),
        "down_w": w[f + "w_down"],
        "uv_w": w[b + "W_uv"],
        "v_b": uv_b[2 * P:4 * P].reshape(1, 2 * P),
        "wo_w": w[b + "W_out"].reshape(2, P, H).transpose(1, 0, 2),
        "router_w": w[f + "router_w"],
    }
    nc = bacc.Bacc("TRN2", target_bir_lowering=False, num_devices=1)
    arrays, args = {}, []
    for name, array in laid.items():
        arrays[name] = np.ascontiguousarray(array)
        args.append(nc.dram_tensor(name, array.shape, mybir.dt.from_np(array.dtype), kind="ExternalInput").ap())
    out = nc.dram_tensor("out", (x.shape[0] * x.shape[1], H), F32, kind="ExternalOutput").ap()
    build(nc, *args, out)
    result = run_bass_kernel_spmd(nc, [arrays], core_ids=[0])
    return result.results[0]["out"].reshape(x.shape)
```

```python
from contextlib import ExitStack

import concourse.bass as bass
from concourse import mybir

ALU = mybir.AluOpType
ACT = mybir.ActivationFunctionType
AX = mybir.AxisListType
F32 = mybir.dt.float32
F32R = mybir.dt.float32r
BF16 = mybir.dt.bfloat16
I32 = mybir.dt.int32
U32 = mybir.dt.uint32

P = 128
H = 128
T = 256
NC = T // P
IT = 2
NS = 16
KC = 4
RK = 64
XP = RK + 2 * NS
NE = 8
FI = 352
NB = -(-FI // P)
FP = NB * P
NP = NE * NB // 2
RING = 6
NDA = 4
NST = 3
EPS = 1e-5
RMS_EPS = 1e-6

V_NS, V_INB, V_CW, V_CB, V_DTB, V_ALOG, V_D, V_OUTB = 0, 1, 5, 13, 15, 17, 49, 51
V_UVB, V_GAMMA, V_BETA, V_WOB, V_END = 52, 55, 57, 59, 60

SEMS = """
 d_vecs d_x d_inw d_xpw d_dtw d_outw d_gate d_up d_down d_uv d_vb d_wo d_rw d_out
 w_zero w_pad w_const w_rows w_sel w_A w_half w_inhi w_inlo w_hi w_lo w_iota v_chain
 m_var m_rstd m_xm m_xt m_hi m_lo m_ph m_eh m_pg m_eg m_g m_conv m_cth m_h m_xp m_xe m_r m_part m_sel m_dt m_z
 m_e m_u m_ln m_delta m_dx m_bc m_dA m_dbx m_scan m_p m_yacc m_y m_yg m_out m_yT m_ot m_x1
 n_var n_rstd n_xm n_xt n_hi n_lo r_lg r_sub r_exp r_w
 f_G f_U f_th f_uc f_a f_in f_dn f_w f_x
 a_pb a_eb a_pu a_eu a_pv a_ev a_b a_qk a_u a_v a_sc a_rl a_sq a_av a_ua a_wo a_woT a_tr a_x
""".split()


SPANS = {
    "first": {"experts": (57.13, 85.29), "in_0": (-72.92, -8.61, 4.59, 6.27, 10.08),
              "scan_0": (18.1, 28.28, 34.79, 42.48), "in_1": (-2.15, 27.46, 31.66, 34.9, 41.74),
              "out_0": (46.4, 49.05), "scan_1": (44.86, 49.98, 73.82, 81.89),
              "in_2": (51.83, 64.33, 69.45, 81.64, 82.64), "out_1": (83.68, 86.5), "norm_0": (49.1, 53.26),
              "route_0": (55.65, 65.44), "norm_1": (87.02, 89.71), "route_1": (108.33, 137.55),
              "select": (-85.61, -85.61), "split_gate": (2.56, 2.56), "split_small": (19.5, 25.43),
              "split_up": (29.54, 29.54)},
    "middle": {"experts": (0, 24.62, 48.08, 73.23, 94.94), "scan_0": (-0.37, 10.79, 24.76, 37.04),
               "in_0": (1.96, 10.07, 16.44, 29.87, 37.37), "out_0": (38.62, 44.76),
               "scan_1": (37.45, 53.26, 69.4, 82.27), "in_1": (46.33, 62.69, 67.16, 76.61, 87.41),
               "out_1": (88.2, 93.45), "attend_0": (-2.46, 6.53, 11, 19.92), "norm_0": (19.97, 24.28),
               "route_0": (25.33, 29.1), "norm_1": (45.09, 48.54), "route_1": (48.54, 52.84),
               "attend_1": (52.96, 61.26, 64.43, 70.25), "norm_2": (70.6, 73.04), "route_2": (76.83, 80.33),
               "norm_3": (94.8, 100.05), "route_3": (148.34, 192.95)},
    "last": {"experts": (0, 25.19, 52.12, 94.51), "attend_0": (-1.41, 5.28, 12.21, 16.48),
             "norm_0": (16.58, 21.32), "route_0": (25.27, 27.16), "attend_1": (34.11, 39.79, 43.18, 49.02),
             "norm_1": (49.75, 49.89), "route_1": (52.16, 68.14)},
}
PAIR_LAGS = {"gate": 0, "up": 0.36, "tanh": 0.5, "up_copy": 0.74, "glu": 0.96, "inner": 1.77}
EXPERT_LAGS = {"down": 2.56, "weigh": 3.44, "add": 4.84}
STATE_LAGS = {"decay": -2.62, "rows": -0.41, "dbx": -0.1, "scan": 0.36, "mulC": 0.72, "sum": 1.28}


def point(span, share):
    parts = len(span) - 1
    k = min(max(int(share * parts), 0), parts - 1)
    return span[k] + (share * parts - k) * (span[k + 1] - span[k])


def place(plan, span, steps):
    for i, step in enumerate(steps):
        plan.append((point(span, i / len(steps)), step))


def mamba_in(p, b):
    return [(name, (p, b)) for name in (
        "m_stats", "m_pow", "m_norm", "m_turn", "m_hi", "m_lo", "m_ph", "m_eh", "m_pg", "m_conv0", "m_eg",
        "m_conv1", "m_g", "m_conv2", "m_conv3", "m_cth", "m_h", "m_xp", "m_xe", "m_r", "m_dt", "m_part", "m_z",
        "m_sel", "m_e", "m_u", "m_ln", "m_c", "m_l", "m_delta", "m_dx")]


def place_scan(plan, u, b, need, span):
    plan.append((span[0], ("rows", (u, b, -1, need))))
    for n in range(NS):
        for name, lag in STATE_LAGS.items():
            if n or name != "sum":
                plan.append((point(span, max(n + lag, 0.01 * n) / NS), (name, (u, b, n, need))))


def mamba_out(u, b):
    return [(name, (u, b)) for name in ("m_skip", "m_gate", "m_out", "m_yT", "m_back", "m_res")]


def last_pair(e):
    return (NB * e + NB - 1) // 2


def norm_steps(l, src, dst, phases=0):
    return [(name, (l, src, dst, phases)) for name in ("n_stats", "n_pow", "n_norm", "n_turn", "n_hi", "n_lo")]


def route_steps(r, w):
    return [(name, (r, w)) for name in ("r_logits", "r_max", "r_exp", "r_prob", "r_top", "r_index", "r_weight")]


def attention_steps(a, b):
    return [(name, (a, b)) for name in (
        "a_pb", "a_eb", "a_pu", "a_b", "a_eu", "a_qk", "a_pv", "a_u", "a_ev", "a_v", "a_sc", "a_rl", "a_sq",
        "a_av", "a_ua", "a_wo", "a_woT", "a_tr", "a_x")]


def place_experts(plan, q, norms, buf, old, new, span):
    for j in range(NP):
        for name, lag in PAIR_LAGS.items():
            plan.append((point(span, (q * NP + j + lag) / (NP * (len(span) - 1))), (name, (q, j, buf, norms))))
    for e in range(NE):
        for name, lag in EXPERT_LAGS.items():
            plan.append((point(span, (q * NP + last_pair(e) + lag) / (NP * (len(span) - 1))),
                         (name, (q, e, buf, old, new))))


def in_order(plan):
    return [step for _, step in sorted(plan, key=lambda entry: entry[0])]


def first_schedule():
    plan, at = [], SPANS["first"]
    place(plan, at["in_0"], [("setup", None)])
    place(plan, at["in_0"], mamba_in(0, 0))
    place_scan(plan, 0, 0, 1, at["scan_0"])
    place(plan, at["in_1"], mamba_in(1, 1))
    place(plan, at["out_0"], mamba_out(0, 0))
    for k, name in enumerate(("select", "split_gate", "split_small", "split_up")):
        place(plan, at[name], [(name, (k,))])
    place_scan(plan, 1, 1, 2, at["scan_1"])
    place(plan, at["norm_0"], norm_steps(0, "x1_0", 1))
    place(plan, at["route_0"], route_steps(0, 1))
    place_experts(plan, 0, 1, 1, "x1_0", "x2_0", at["experts"])
    place(plan, at["in_2"], mamba_in(2, 0))
    place(plan, at["out_1"], mamba_out(1, 1))
    place(plan, at["norm_1"], norm_steps(1, "x1_1", 0))
    place(plan, at["route_1"], route_steps(1, 0))
    return in_order(plan)


def middle_schedule():
    plan, at = [], SPANS["middle"]
    for q, (norms, buf, old, new) in enumerate(((0, 0, "x1_1", "x2_1"), (2, 1, "x2_0", "x3_0"),
                                                (3, 0, "x1_0", "x2_0"), (5, 1, "x2_1", "x3_1"))):
        place_experts(plan, q, norms, buf, old, new, at["experts"])
    for u in range(2):
        place_scan(plan, u, u, u, at[f"scan_{u}"])
        place(plan, at[f"in_{u}"], mamba_in(u, 1 - u))
        place(plan, at[f"out_{u}"], mamba_out(u, u))
    place(plan, at["attend_0"], norm_steps(0, "x2_0", "A") + attention_steps(0, 0))
    place(plan, at["norm_0"], norm_steps(1, "x2_0", 1))
    place(plan, at["norm_1"], norm_steps(2, "x1_0", 0))
    place(plan, at["attend_1"], norm_steps(3, "x2_1", "A", 1) + attention_steps(1, 1))
    place(plan, at["norm_2"], norm_steps(4, "x2_1", 1))
    place(plan, at["norm_3"], norm_steps(5, "x1_1", 0))
    for r in range(4):
        place(plan, at[f"route_{r}"], route_steps(r, 1 - r % 2))
    return in_order(plan)


def last_schedule():
    plan, at = [], SPANS["last"]
    for q, (norms, buf, old, new) in enumerate(((0, 0, "x1_1", "x2_1"), (2, 1, "x2_0", "x3_0"),
                                                (4, 0, "x2_1", "x3_1"))):
        place_experts(plan, q, norms, buf, old, new, at["experts"])
    place(plan, at["attend_0"], norm_steps(0, "x2_0", "A") + attention_steps(0, 0))
    place(plan, at["norm_0"], norm_steps(1, "x2_0", 1))
    place(plan, at["attend_1"], norm_steps(2, "x2_1", "A", 1) + attention_steps(1, 1))
    place(plan, at["norm_1"], norm_steps(3, "x2_1", 0))
    for r in range(2):
        place(plan, at[f"route_{r}"], route_steps(r, 1 - r % 2))
    return in_order(plan)


def build(nc, x, vecs, in_w, xproj_w, dt_w, out_w, gate_w, up_w, down_w, uv_w, v_b, wo_w, router_w, out):
    sequences = x.shape[0] // T
    with ExitStack() as ctx:
        def sb(name, shape, dt=F32):
            return ctx.enter_context(nc.sbuf_tensor(name, shape, dt))

        def two(bank):
            return bank.rearrange("p (a t) -> p a t", a=2)

        ps = ctx.enter_context(nc.psum_tensor("ps", [P, 8, 512], F32))
        s = {n: ctx.enter_context(nc.semaphore(n)) for n in SEMS}
        rowps = [two(ps[:, k, :]) for k in range(2)]
        psG, psU, psO = [two(ps[:, 2 + k, :]) for k in range(2)], two(ps[:, 4, :]), ps[:, 5, 0:NC * H]
        chainps, mambaps = ps[:, 6, :], ps[:, 7, :]

        ident = sb("ident", [P, P])
        sel = sb("sel", [96, 2 * NS, P], BF16)
        select_rows = sb("select_rows", [96, 2 * NS])
        ones_row = sb("ones_row", [1, P])
        neghalf = sb("neghalf", [P, NC])
        iota_i = sb("iota_i", [P, NE], I32)
        iota8 = sb("iota8", [P, NE])
        vec = sb("vec", [P, V_END])
        half = sb("half", [P, V_END])
        qvec = sb("qvec", [P, 2])
        A = sb("A", [P, IT, NS])
        inw_hi = sb("inw_hi", [P, 512], F32R)
        inw_lo = sb("inw_lo", [P, 512], F32R)
        xpw = sb("xpw", [P, IT, XP])
        dtw = sb("dtw", [RK, IT * P])
        outw = sb("outw", [P, IT, H])
        gate_hi = sb("gate_hi", [P, NE * FP], F32R)
        gate_lo = sb("gate_lo", [P, NE * FP], F32R)
        up_hi = sb("up_hi", [P, NE * FP], F32R)
        up_lo = sb("up_lo", [P, NE * FP], F32R)
        down = sb("down", [P, NE, NB, H])
        uv_hi = sb("uv_hi", [P, 640], F32R)
        uv_lo = sb("uv_lo", [P, 640], F32R)
        vb_row = sb("vb_row", [1, 2 * P])
        wo = sb("wo", [P, 2, H])
        rw_raw = sb("rw_raw", [P, NE])
        rw_hi = sb("rw_hi", [P, NE], F32R)
        rw_lo = sb("rw_lo", [P, NE], F32R)

        xin = sb("xin", [P, 2, NC, H])
        m_bn = sb("m_bn", [P, NC, 6])
        m_mv = sb("m_mv", [P, NC, 2])
        m_ve = sb("m_ve", [P, NC])
        m_r = sb("m_r", [P, NC])
        m_xn = sb("m_xn", [P, NC, H])
        m_xhi = sb("m_xhi", [P, T], F32R)
        m_xlo = sb("m_xlo", [P, T], F32R)
        xpad = sb("xpad", [P, IT, T + KC - 1])
        conv = sb("conv", [P, IT, T])
        conv_th = sb("conv_th", [P, IT, T])
        h = sb("h", [P, 2, IT, T])
        gate_z = sb("gate_z", [P, IT, T])
        gate_th = sb("gate_th", [P, IT, T])
        gact = sb("gact", [P, 2, IT, T])
        ts = sb("ts", [RK, T])
        bc_r = sb("bc_r", [96, T])
        bc_s = sb("bc_s", [96, 2, T], BF16)
        sp_z = sb("sp_z", [P, IT, T])
        sp_e = sb("sp_e", [P, IT, T])
        sp_u = sb("sp_u", [P, IT, T])
        sp_ln = sb("sp_ln", [P, IT, T])
        delta = sb("delta", [P, 2, IT, T])
        dx = sb("dx", [P, 2, IT, T])
        dA = sb("dA", [P, NDA, IT, T])
        dbx_in = sb("dbx_in", [P, 2, IT, T])
        st = sb("st", [P, NST, IT, T])
        yacc = sb("yacc", [P, 2, IT, T])
        yT = sb("yT", [P, T])

        xs = {f"x{k}_{b}": sb(f"x{k}_{b}", [P, NC, H]) for k in (1, 2, 3) for b in (0, 1)}

        n_bn = sb("n_bn", [P, NC, 6])
        n_mv = sb("n_mv", [P, NC, 2])
        n_ve = sb("n_ve", [P, NC])
        n_r = sb("n_r", [P, NC])
        n_xn = sb("n_xn", [P, NC, H])
        xhi = {k: sb(f"xhi_{k}", [P, T], F32R) for k in (0, 1, "A")}
        xlo = {k: sb(f"xlo_{k}", [P, T], F32R) for k in (0, 1, "A")}
        lg_mx = sb("lg_mx", [P, NC])
        lg = sb("lg", [P, NC, NE])
        lg_exp = sb("lg_exp", [P, NC, NE])
        prob = sb("prob", [P, NC, NE])
        total = sb("total", [P, NC])
        total_r = sb("total_r", [P, NC])
        top8 = sb("top8", [P, NC, 8])
        idx8 = sb("idx8", [P, NC, 8], U32)
        idxf = sb("idxf", [P, NC, 2])
        den = sb("den", [P, NC])
        den_r = sb("den_r", [P, NC])
        w2 = sb("w2", [P, NC, 2])
        spread_w = sb("spread_w", [P, NC, 2, NE])
        wts = sb("wts", [P, 2, NC, NE])

        th = sb("th", [P, 2, 2, T])
        uc = sb("uc", [P, 2, 2, T])
        ga = sb("ga", [P, 2, 2, T])
        staging = sb("staging", [P, NE * FP])
        inner = staging[:].rearrange("p (r b t) -> p r b t", r=RING, b=2)
        raw = staging[:].rearrange("p (e f) -> p e f", e=NE)

        weighted = sb("weighted", [P, 2, NC, H])

        at_bz, at_bt, at_base = sb("at_bz", [P, T]), sb("at_bt", [P, T]), sb("at_base", [P, T])
        at_q, at_k = sb("at_q", [P, T]), sb("at_k", [P, T])
        at_uzt = sb("at_uzt", [P, 2, 2, T])
        at_uz, at_ut, at_u = at_uzt[:, 0], at_uzt[:, 1], sb("at_u", [P, 2, T])
        at_v = sb("at_v", [P, NC, 2 * P])
        at_s = sb("at_s", [P, 2, T])
        inw_raw = at_v[:].rearrange("p c e -> p (c e)")
        uv_raw = at_uzt[:].rearrange("p i a t -> p (i a t)")[:, 0:640]
        at_oT = sb("at_oT", [P, T])

        def v(col, n=1):
            return vec[:, col:col + n]

        def hv(col):
            return half[:, col:col + 1]

        def run_schedule(share, schedule):
            for name, arg in schedule:
                if name in share:
                    share[name](arg)

        def block_of(ctx2, schedule, loads, stores, first):
            block = ctx2.enter_context(nc.Block())

            @block.sync
            def _(sp):
                def load(k):
                    row, b, before = loads[k]
                    if before:
                        sp.wait_ge(s["m_x1"], before)
                    rows = x[bass.ds(row * T, T), :]
                    sp.dma_start(xin[:, b], rows.rearrange("(c p) h -> p c h", p=P)).then_inc(s["d_x"], 16)

                if first:
                    sp.dma_start(vec[:], vecs).then_inc(s["d_vecs"], 16)
                    load(0)
                    load(1)
                    for sem, dst, src in (("d_inw", inw_raw, in_w), ("d_xpw", xpw[:], xproj_w),
                                          ("d_dtw", dtw[:], dt_w), ("d_outw", outw[:], out_w),
                                          ("d_uv", uv_raw, uv_w), ("d_rw", rw_raw[:], router_w),
                                          ("d_vb", vb_row[:], v_b), ("d_wo", wo[:], wo_w)):
                        sp.dma_start(dst, src).then_inc(s[sem], 16)
                    experts = "h (e f) -> h e f"
                    sp.dma_start(raw[:, :, 0:FI], gate_w.rearrange(experts, e=NE)).then_inc(s["d_gate"], 16)
                    for k in range(NB):
                        rows = min(P, FI - k * P)
                        sp.dma_start(down[0:rows, :, k, :],
                                     down_w[:, k * P:k * P + rows, :].rearrange("e p h -> p e h")).then_inc(s["d_down"], 16)
                    sp.wait_ge(s["w_lo"], 1)
                    sp.dma_start(raw[:, :, 0:FI], up_w.rearrange(experts, e=NE)).then_inc(s["d_up"], 16)
                    load(2)
                    sp.wait_ge(s["d_vb"], 16)
                    sp.wait_ge(s["d_wo"], 16)
                else:
                    for k in range(len(loads)):
                        load(k)
                for k, (count, row, name) in enumerate(stores):
                    sp.wait_ge(s["f_x"], NE * count)
                    rows = out[bass.ds(row * T, T), :]
                    sp.dma_start(rows.rearrange("(c p) h -> p c h", p=P), xs[name][:]).then_inc(s["d_out"], 16)
                if stores:
                    sp.wait_ge(s["d_out"], 16 * len(stores))

            @block.gpsimd
            def _(pool):
                def setup(_):
                    nc.gpsimd.memset(ident[:], 0.0).then_inc(s["w_zero"], 1)
                    pool.wait_ge(s["w_zero"], 1)
                    nc.gpsimd.affine_select(out=ident[:], in_=ident[:], compare_op=ALU.not_equal, fill=1.0, base=0,
                                            pattern=[[-1, P]], channel_multiplier=1).then_inc(s["w_const"], 1)
                    nc.gpsimd.memset(neghalf[:], -0.5).then_inc(s["w_zero"], 1)
                    nc.gpsimd.iota(iota_i[:], pattern=[[1, NE]], base=0, channel_multiplier=0).then_inc(s["w_iota"], 1)
                    nc.gpsimd.memset(raw[:, :, FI:FP], 0.0).then_inc(s["w_pad"], 1)
                    nc.gpsimd.memset(ones_row[:], 1.0)
                    pool.wait_ge(s["w_zero"], 2)

                def remainder(n, lo, whole, hi):
                    pool.wait_ge(s["w_hi"], n)
                    nc.gpsimd.tensor_tensor(lo[:], whole, hi[:].bitcast(F32), ALU.subtract).then_inc(s["w_lo"], 1)

                def split_gate(_):
                    remainder(1, gate_lo, staging[:], gate_hi)

                def split_small(_):
                    remainder(2, uv_lo, uv_raw, uv_hi)
                    remainder(3, rw_lo, rw_raw[:], rw_hi)

                def split_up(_):
                    remainder(4, up_lo, staging[:], up_hi)

                def m_pow(arg):
                    pool.wait_ge(s["m_var"], arg[0] + 1)
                    nc.gpsimd.tensor_tensor(m_r[:], m_ve[:], neghalf[:], ALU.pow).then_inc(s["m_rstd"], 1)

                def n_pow(arg):
                    pool.wait_ge(s["n_var"], arg[0] + 1)
                    nc.gpsimd.tensor_tensor(n_r[:], n_ve[:], neghalf[:], ALU.pow).then_inc(s["n_rstd"], 1)

                def m_dx(arg):
                    p, b = arg
                    pool.wait_ge(s["m_delta"], p + 1)
                    nc.gpsimd.tensor_tensor(dx[:, b], delta[:, b], h[:, b], ALU.mult).then_inc(s["m_dx"], 1)

                def sum_states(arg):
                    u, b, n, _ = arg
                    i = u * NS + n
                    pool.wait_ge(s["m_p"], i + 1)
                    if n > 1:
                        pool.wait_ge(s["m_yacc"], u * (NS - 1) + n - 1)
                    nc.gpsimd.tensor_tensor(yacc[:, b], st[:, (i - 1) % NST] if n == 1 else yacc[:, b], st[:, i % NST],
                                            ALU.add).then_inc(s["m_yacc"], 1)

                def m_gate(arg):
                    u, b = arg
                    pool.wait_ge(s["m_y"], u + 1)
                    nc.gpsimd.tensor_tensor(yacc[:, b], yacc[:, b], gact[:, b], ALU.mult).then_inc(s["m_yg"], 1)

                def inner_step(arg):
                    q, j, *_ = arg
                    k = q * NP + j
                    pool.wait_ge(s["f_a"], k + 1)
                    pool.wait_ge(s["f_uc"], k + 1)
                    if k >= RING:
                        old_q, old_j = divmod(k - RING, NP)
                        pool.wait_ge(s["f_dn"], old_q * NE + (2 * old_j + 1) // NB + 1)
                    nc.gpsimd.tensor_tensor(inner[:, k % RING], ga[:, k % 2], uc[:, k % 2], ALU.mult).then_inc(s["f_in"], 1)

                def add(arg):
                    q, e, _, old, new = arg
                    k = q * NE + e
                    pool.wait_ge(s["f_w"], k + 1)
                    if e:
                        pool.wait_ge(s["f_x"], k)
                    nc.gpsimd.tensor_tensor(xs[new][:], xs[new if e else old][:], weighted[:, k % 2],
                                            ALU.add).then_inc(s["f_x"], 1)

                run_schedule({"setup": setup, "split_gate": split_gate,
                              "split_small": split_small, "split_up": split_up, "m_pow": m_pow, "n_pow": n_pow,
                              "m_dx": m_dx, "sum": sum_states, "m_gate": m_gate, "inner": inner_step, "add": add}, schedule)

            @block.scalar
            def _(act):
                def setup(_):
                    act.wait_ge(s["d_vecs"], 16)
                    nc.scalar.activation(A[:].rearrange("p a n -> p (a n)"), v(V_ALOG, IT * NS), ACT.Exp).then_inc(s["w_A"], 1)
                    act.wait_ge(s["d_inw"], 16)
                    nc.scalar.copy(inw_hi[:], inw_raw).then_inc(s["w_inhi"], 1)
                    act.wait_ge(s["w_half"], 1)

                def select(_):
                    act.wait_ge(s["w_rows"], 2)
                    nc.scalar.copy(sel[:], select_rows[:].unsqueeze(2).broadcast_to([96, 2 * NS, P])).then_inc(s["w_sel"], 1)

                def float32r_part(sem, whole, hi):
                    act.wait_ge(s[sem], 16)
                    nc.scalar.copy(hi[:], whole).then_inc(s["w_hi"], 1)

                def split_gate(_):
                    act.wait_ge(s["w_pad"], 1)
                    float32r_part("d_gate", staging[:], gate_hi)

                def split_small(_):
                    float32r_part("d_uv", uv_raw, uv_hi)
                    float32r_part("d_rw", rw_raw[:], rw_hi)

                def split_up(_):
                    float32r_part("d_up", staging[:], up_hi)

                def m_hi(arg):
                    act.wait_ge(s["m_xt"], arg[0] + 1)
                    nc.scalar.activation(m_xhi[:], mambaps[:, 0:T], ACT.Copy, scale=v(V_NS)).then_inc(s["m_hi"], 1)

                def m_eh(arg):
                    act.wait_ge(s["m_ph"], arg[0] + 1)
                    for it in range(IT):
                        ins = nc.scalar.activation(xpad[:, it, KC - 1:], two(mambaps)[:, it], ACT.Identity,
                                                   bias=v(V_INB + it))
                    ins.then_inc(s["m_eh"], 1)

                def m_eg(arg):
                    act.wait_ge(s["m_pg"], arg[0] + 1)
                    for it in range(IT):
                        bias = hv(V_INB + IT + it)
                        nc.scalar.activation(gate_z[:, it], two(mambaps)[:, it], ACT.Identity, bias=bias, scale=0.5)
                        ins = nc.scalar.activation(gate_th[:, it], two(mambaps)[:, it], ACT.Tanh, bias=bias, scale=0.5)
                    ins.then_inc(s["m_eg"], 1)

                def m_cth(arg):
                    act.wait_ge(s["m_conv"], arg[0] + 1)
                    nc.scalar.activation(conv_th[:], conv[:], ACT.Tanh).then_inc(s["m_cth"], 1)

                def m_xe(arg):
                    act.wait_ge(s["m_xp"], arg[0] + 1)
                    nc.scalar.copy(bc_s[64:96, arg[1]], mambaps[64:96, 0:T])
                    nc.scalar.copy(ts[:], mambaps[0:RK, 0:T]).then_inc(s["m_xe"], 1)

                def m_part(arg):
                    act.wait_ge(s["m_r"], arg[0] + 1)
                    nc.scalar.copy(bc_s[32:64, arg[1]], bc_r[32:64, :]).then_inc(s["m_part"], 1)

                def m_z(arg):
                    act.wait_ge(s["m_dt"], arg[0] + 1)
                    for it in range(IT):
                        nc.scalar.activation(sp_e[:, it], two(mambaps)[:, it], ACT.Abs, bias=v(V_DTB + it))
                        ins = nc.scalar.activation(sp_z[:, it], two(mambaps)[:, it], ACT.Identity, bias=v(V_DTB + it))
                    ins.then_inc(s["m_z"], 1)

                def m_e(arg):
                    act.wait_ge(s["m_z"], arg[0] + 1)
                    nc.scalar.activation(sp_e[:], sp_e[:], ACT.Exp, scale=-1.0).then_inc(s["m_e"], 1)

                def m_u(arg):
                    act.wait_ge(s["m_e"], arg[0] + 1)
                    nc.scalar.activation(sp_u[:], sp_e[:], ACT.Copy, bias=1.0).then_inc(s["m_u"], 1)

                def m_ln(arg):
                    act.wait_ge(s["m_u"], arg[0] + 1)
                    nc.scalar.activation(sp_ln[:], sp_u[:], ACT.Ln).then_inc(s["m_ln"], 1)

                def decay(arg):
                    u, b, n, need = arg
                    i = u * NS + n
                    if need:
                        act.wait_ge(s["m_delta"], need)
                    if i >= NDA:
                        act.wait_ge(s["m_scan"], i - NDA + 1)
                    for it in range(IT):
                        ins = nc.scalar.activation(dA[:, i % NDA, it, 1:], delta[:, b, it, 1:], ACT.Exp,
                                                   scale=A[:, it, n:n + 1])
                    ins.then_inc(s["m_dA"], 1)

                def m_yT(arg):
                    act.wait_ge(s["m_out"], arg[0] + 1)
                    nc.scalar.activation(yT[:], mambaps[:, 0:T], ACT.Identity, bias=v(V_OUTB)).then_inc(s["m_yT"], 1)

                def n_hi(arg):
                    l, _, dst, _ = arg
                    act.wait_ge(s["n_xt"], l + 1)
                    nc.scalar.copy(xhi[dst][:], chainps[:, 0:T]).then_inc(s["n_hi"], 1)

                def r_exp(arg):
                    act.wait_ge(s["r_sub"], arg[0] + 1)
                    nc.scalar.activation(lg_exp[:], lg[:], ACT.Exp).then_inc(s["r_exp"], 1)

                def tanh(arg):
                    q, j, *_ = arg
                    k = q * NP + j
                    act.wait_ge(s["f_G"], k + 1)
                    if k >= 2:
                        act.wait_ge(s["f_a"], k - 1)
                    nc.scalar.activation(th[:, k % 2], psG[k % 2], ACT.Tanh, scale=0.5).then_inc(s["f_th"], 1)

                def up_copy(arg):
                    q, j, *_ = arg
                    k = q * NP + j
                    act.wait_ge(s["f_U"], k + 1)
                    if k >= 2:
                        act.wait_ge(s["f_in"], k - 1)
                    nc.scalar.copy(uc[:, k % 2], psU).then_inc(s["f_uc"], 1)

                def weigh(arg):
                    q, e, buf, *_ = arg
                    k = q * NE + e
                    act.wait_ge(s["f_dn"], k + 1)
                    if e == 0 and q + first:
                        act.wait_ge(s["r_w"], q + first)
                    if k >= 2:
                        act.wait_ge(s["f_x"], k - 1)
                    for c in range(NC):
                        ins = nc.scalar.activation(weighted[:, k % 2, c, :], psO[:, c * H:(c + 1) * H], ACT.Copy,
                                                   scale=wts[:, buf, c, e:e + 1])
                    ins.then_inc(s["f_w"], 1)

                def a_eb(arg):
                    act.wait_ge(s["a_pb"], arg[0] + 1)
                    bias = hv(V_UVB + 2)
                    nc.scalar.activation(at_bz[:], chainps[:, 0:T], ACT.Identity, bias=bias, scale=0.5)
                    nc.scalar.activation(at_bt[:], chainps[:, 0:T], ACT.Tanh, bias=bias, scale=0.5).then_inc(s["a_eb"], 1)

                def a_eu(arg):
                    act.wait_ge(s["a_pu"], arg[0] + 1)
                    for a in range(2):
                        bias = hv(V_UVB + a)
                        nc.scalar.activation(at_uz[:, a], two(chainps)[:, a], ACT.Identity, bias=bias, scale=0.5)
                        ins = nc.scalar.activation(at_ut[:, a], two(chainps)[:, a], ACT.Tanh, bias=bias, scale=0.5)
                    ins.then_inc(s["a_eu"], 1)

                def a_ev(arg):
                    act.wait_ge(s["a_pv"], arg[0] + 1)
                    nc.scalar.activation(at_v[:], two(chainps), ACT.Tanh, scale=0.5).then_inc(s["a_ev"], 1)

                def a_rl(arg):
                    act.wait_ge(s["a_sc"], arg[0] + 1)
                    nc.scalar.activation(at_s[:], two(chainps), ACT.Relu).then_inc(s["a_rl"], 1)

                def a_sq(arg):
                    act.wait_ge(s["a_rl"], arg[0] + 1)
                    nc.scalar.activation(at_s[:], at_s[:], ACT.Square).then_inc(s["a_sq"], 1)

                def a_woT(arg):
                    act.wait_ge(s["a_wo"], arg[0] + 1)
                    nc.scalar.activation(at_oT[:], chainps[:, 0:T], ACT.Identity, bias=v(V_WOB)).then_inc(s["a_woT"], 1)

                run_schedule({"setup": setup, "select": select, "split_gate": split_gate,
                              "split_small": split_small, "split_up": split_up, "m_hi": m_hi,
                              "m_eh": m_eh, "m_eg": m_eg, "m_cth": m_cth, "m_xe": m_xe, "m_part": m_part, "m_z": m_z, "m_e": m_e, "m_u": m_u,
                              "m_ln": m_ln, "decay": decay, "m_yT": m_yT, "n_hi": n_hi, "r_exp": r_exp, "tanh": tanh,
                              "up_copy": up_copy, "weigh": weigh, "a_eb": a_eb, "a_eu": a_eu, "a_ev": a_ev, "a_rl": a_rl, "a_sq": a_sq,
                              "a_woT": a_woT}, schedule)

            @block.vector
            def _(dve):
                chain = [0]

                def mark(ins):
                    chain[0] += 1
                    ins.then_inc(s["v_chain"], 1)
                    return chain[0]

                def link():
                    dve.wait_ge(s["v_chain"], chain[0])

                def setup(_):
                    mark(nc.vector.memset(xpad[:, :, 0:KC - 1], 0.0))
                    mark(nc.vector.memset(dA[:, :, :, 0:1].rearrange("p n a o -> p (n a) o"), 0.0))
                    dve.wait_ge(s["w_iota"], 1)
                    mark(nc.vector.tensor_copy(iota8[:], iota_i[:]))
                    dve.wait_ge(s["d_vecs"], 16)
                    nc.vector.tensor_scalar(half[:], vec[:], 0.5, None, ALU.mult).then_inc(s["w_half"], 1)
                    mark(nc.vector.tensor_scalar(qvec[:, 0:1], v(V_GAMMA), 1.0 / T, None, ALU.mult))
                    mark(nc.vector.tensor_scalar(qvec[:, 1:2], v(V_BETA), 1.0 / T, None, ALU.mult))
                    dve.wait_ge(s["w_A"], 1)
                    a = A[:].rearrange("p a n -> p (a n)")
                    nc.vector.tensor_scalar(a, a, -1.0, None, ALU.mult).then_inc(s["w_A"], 1)
                    dve.wait_ge(s["w_inhi"], 1)
                    nc.vector.tensor_tensor(inw_lo[:], inw_raw, inw_hi[:].bitcast(F32), ALU.subtract).then_inc(s["w_inlo"], 1)

                def select(_):
                    dve.wait_ge(s["w_const"], 1)
                    nc.vector.tensor_tensor(select_rows[:], ident[0:96, 0:32], ident[0:96, 32:64], ALU.add).then_inc(s["w_rows"], 1)
                    dve.wait_ge(s["w_rows"], 1)
                    nc.vector.tensor_tensor(select_rows[:], select_rows[:], ident[0:96, 64:96], ALU.add).then_inc(s["w_rows"], 1)

                def norm_stats(xt, bn, mv):
                    for c in range(NC):
                        mark(nc.vector.bn_stats(bn[:, c, :], xt[:, c, :]))
                    link()
                    for c in range(NC):
                        mark(nc.vector.bn_aggr(mv[:, c, :], bn[:, c, :]))
                    link()

                def m_stats(arg):
                    p, b = arg
                    dve.wait_ge(s["d_x"], 16 * (p + 1))
                    norm_stats(xin[:, b], m_bn, m_mv)
                    nc.vector.tensor_scalar(m_ve[:], m_mv[:, :, 1], 1.0 + RMS_EPS, RMS_EPS * EPS,
                                            ALU.mult, ALU.add).then_inc(s["m_var"], 1)

                def m_norm(arg):
                    p, b = arg
                    dve.wait_ge(s["m_rstd"], p + 1)
                    for c in range(NC):
                        ins = nc.vector.tensor_scalar(m_xn[:, c, :], xin[:, b, c, :], m_mv[:, c, 0:1], m_r[:, c:c + 1],
                                                      ALU.subtract, ALU.mult)
                    ins.then_inc(s["m_xm"], 1)

                def m_lo(arg):
                    dve.wait_ge(s["m_hi"], arg[0] + 1)
                    nc.vector.scalar_tensor_tensor(out=m_xlo[:], in0=mambaps[:, 0:T], scalar=v(V_NS),
                                                   in1=m_xhi[:].bitcast(F32), op0=ALU.mult,
                                                   op1=ALU.subtract).then_inc(s["m_lo"], 1)

                conv_mark = [0]

                def conv_tap(k):
                    def tap(arg):
                        if k == 0:
                            dve.wait_ge(s["m_eh"], arg[0] + 1)
                        else:
                            dve.wait_ge(s["v_chain"], conv_mark[0])
                        for it in range(IT):
                            w, src, dst = hv(V_CW + it * KC + k), xpad[:, it, k:k + T], conv[:, it]
                            if k == 0:
                                ins = nc.vector.tensor_scalar(dst, src, w, hv(V_CB + it), ALU.mult, ALU.add)
                            else:
                                ins = nc.vector.scalar_tensor_tensor(out=dst, in0=src, scalar=w, in1=dst,
                                                                     op0=ALU.mult, op1=ALU.add)
                            if k < KC - 1:
                                conv_mark[0] = mark(ins)
                        if k == KC - 1:
                            ins.then_inc(s["m_conv"], 1)
                    return tap

                def m_g(arg):
                    p, b = arg
                    dve.wait_ge(s["m_eg"], p + 1)
                    nc.vector.scalar_tensor_tensor(out=gact[:, b], in0=gate_th[:], scalar=1.0, in1=gate_z[:],
                                                   op0=ALU.add, op1=ALU.mult).then_inc(s["m_g"], 1)

                def m_h(arg):
                    p, b = arg
                    dve.wait_ge(s["m_cth"], p + 1)
                    nc.vector.scalar_tensor_tensor(out=h[:, b], in0=conv_th[:], scalar=1.0, in1=conv[:],
                                                   op0=ALU.add, op1=ALU.mult).then_inc(s["m_h"], 1)

                def rest(arg):
                    dve.wait_ge(s["m_xe"], arg[0] + 1)
                    nc.vector.tensor_tensor(bc_r[32:64, :], mambaps[64:96, 0:T], bc_s[64:96, arg[1]],
                                            ALU.subtract).then_inc(s["m_r"], 1)

                def m_sel(arg):
                    b = arg[1]
                    dve.wait_ge(s["m_part"], arg[0] + 1)
                    nc.vector.tensor_tensor(bc_s[0:32, b], bc_r[32:64, :], bc_s[32:64, b], ALU.subtract).then_inc(s["m_sel"], 1)

                sp_mark = [0]

                def m_c(arg):
                    dve.wait_ge(s["m_u"], arg[0] + 1)
                    sp_mark[0] = mark(nc.vector.scalar_tensor_tensor(out=sp_e[:], in0=sp_u[:], scalar=-1.0, in1=sp_e[:],
                                                                     op0=ALU.add, op1=ALU.subtract))

                def m_l(arg):
                    dve.wait_ge(s["v_chain"], sp_mark[0])
                    dve.wait_ge(s["m_ln"], arg[0] + 1)
                    sp_mark[0] = mark(nc.vector.tensor_tensor(sp_e[:], sp_ln[:], sp_e[:], ALU.subtract))

                def m_delta(arg):
                    dve.wait_ge(s["v_chain"], sp_mark[0])
                    nc.vector.scalar_tensor_tensor(out=delta[:, arg[1]], in0=sp_z[:], scalar=0.0, in1=sp_e[:],
                                                   op0=ALU.max, op1=ALU.add).then_inc(s["m_delta"], 1)

                def dbx(arg):
                    u, b, n, need = arg
                    i = u * NS + n
                    if need:
                        dve.wait_ge(s["m_dx"], need)
                    r = u * (NS + 1) + n
                    dve.wait_ge(s["m_bc"], r + 1)
                    if i > 1:
                        dve.wait_ge(s["m_scan"], i - 1)
                    nc.vector.tensor_tensor(dbx_in[:, i % 2], dx[:, b], rowps[r % 2][:, 0:1].broadcast_to([P, IT, T]),
                                            ALU.mult).then_inc(s["m_dbx"], 1)

                def scan(arg):
                    u, b, n, _ = arg
                    i = u * NS + n
                    dve.wait_ge(s["m_dA"], i + 1)
                    dve.wait_ge(s["m_dbx"], i + 1)
                    if i >= NST:
                        old_u, old_n = divmod(i - NST, NS)
                        dve.wait_ge(s["m_yacc"], old_u * (NS - 1) + max(1, old_n))
                    nc.vector.tensor_tensor_scan(out=st[:, i % NST].rearrange("p a t -> p (a t)"),
                                                 data0=dA[:, i % NDA].rearrange("p a t -> p (a t)"),
                                                 data1=dbx_in[:, i % 2].rearrange("p a t -> p (a t)"), initial=0.0,
                                                 op0=ALU.mult, op1=ALU.add).then_inc(s["m_scan"], 1)

                def mulC(arg):
                    u, b, n, _ = arg
                    i = u * NS + n
                    r = u * (NS + 1) + n + 1
                    dve.wait_ge(s["m_bc"], r + 1)
                    dve.wait_ge(s["m_scan"], i + 1)
                    nc.vector.tensor_tensor(st[:, i % NST], st[:, i % NST], rowps[r % 2][:, 1:2].broadcast_to([P, IT, T]),
                                            ALU.mult).then_inc(s["m_p"], 1)

                def m_skip(arg):
                    u, b = arg
                    dve.wait_ge(s["m_yacc"], (u + 1) * (NS - 1))
                    for it in range(IT):
                        ins = nc.vector.scalar_tensor_tensor(out=yacc[:, b, it], in0=h[:, b, it], scalar=v(V_D + it),
                                                             in1=yacc[:, b, it], op0=ALU.mult, op1=ALU.add)
                    ins.then_inc(s["m_y"], 1)

                def m_res(arg):
                    u, b = arg
                    dve.wait_ge(s["m_ot"], u + 1)
                    nc.vector.tensor_tensor(xs[f"x1_{b}"][:], xin[:, b], two(mambaps[:, T:2 * T]), ALU.add).then_inc(s["m_x1"], 1)
                    dve.wait_ge(s["m_x1"], u + 1)

                def n_stats(arg):
                    l, src, _, phases = arg
                    if phases:
                        dve.wait_ge(s["f_x"], NE * phases)
                    norm_stats(xs[src], n_bn, n_mv)
                    nc.vector.tensor_scalar(n_ve[:], n_mv[:, :, 1], EPS, None, ALU.add).then_inc(s["n_var"], 1)

                def n_norm(arg):
                    l, src, *_ = arg
                    dve.wait_ge(s["n_rstd"], l + 1)
                    for c in range(NC):
                        ins = nc.vector.tensor_scalar(n_xn[:, c, :], xs[src][:, c, :], n_mv[:, c, 0:1], n_r[:, c:c + 1],
                                                      ALU.subtract, ALU.mult)
                    ins.then_inc(s["n_xm"], 1)

                def n_lo(arg):
                    l, _, dst, _ = arg
                    dve.wait_ge(s["n_hi"], l + 1)
                    nc.vector.tensor_tensor(xlo[dst][:], chainps[:, 0:T], xhi[dst][:].bitcast(F32),
                                            ALU.subtract).then_inc(s["n_lo"], 1)

                def wide(a, n):
                    return a[:].unsqueeze(2).broadcast_to([P, NC, n])

                def each(a):
                    return a[:].unsqueeze(3).broadcast_to([P, NC, 2, NE])

                def r_max(arg):
                    dve.wait_ge(s["r_lg"], arg[0] + 1)
                    logits = chainps[:, T:T + NC * NE].rearrange("p (c e) -> p c e", c=NC)
                    mark(nc.vector.reduce_max(lg_mx[:], logits, AX.X))
                    link()
                    nc.vector.tensor_tensor(lg[:], logits, wide(lg_mx, NE), ALU.subtract).then_inc(s["r_sub"], 1)

                def r_prob(arg):
                    dve.wait_ge(s["r_exp"], arg[0] + 1)
                    mark(nc.vector.tensor_reduce(total[:], lg_exp[:], AX.X, ALU.add))
                    link()
                    mark(nc.vector.reciprocal(total_r[:], total[:]))
                    link()
                    mark(nc.vector.tensor_tensor(prob[:], lg_exp[:], wide(total_r, NE), ALU.mult))

                def r_top(arg):
                    link()
                    for c in range(NC):
                        mark(nc.vector.max(top8[:, c, :], prob[:, c, :]))

                def r_index(arg):
                    link()
                    for c in range(NC):
                        mark(nc.vector.max_index(idx8[:, c, :], top8[:, c, :], prob[:, c, :]))
                    mark(nc.vector.tensor_tensor(den[:], top8[:, :, 0], top8[:, :, 1], ALU.add))
                    link()
                    mark(nc.vector.tensor_copy(idxf[:], idx8[:, :, 0:2]))
                    mark(nc.vector.reciprocal(den_r[:], den[:]))
                    link()
                    expert = iota8[:].unsqueeze(1).unsqueeze(1).broadcast_to([P, NC, 2, NE])
                    mark(nc.vector.tensor_tensor(spread_w[:], expert, each(idxf), ALU.is_equal))

                def r_weight(arg):
                    _, w = arg
                    link()
                    mark(nc.vector.scalar_tensor_tensor(out=w2[:], in0=top8[:, :, 0:2], scalar=0.5, in1=wide(den_r, 2),
                                                        op0=ALU.mult, op1=ALU.mult))
                    link()
                    mark(nc.vector.tensor_tensor(spread_w[:], spread_w[:], each(w2), ALU.mult))
                    link()
                    nc.vector.tensor_tensor(wts[:, w], spread_w[:, :, 0], spread_w[:, :, 1], ALU.add).then_inc(s["r_w"], 1)

                def glu(arg):
                    q, j, *_ = arg
                    k = q * NP + j
                    dve.wait_ge(s["f_th"], k + 1)
                    if k >= 2:
                        dve.wait_ge(s["f_in"], k - 1)
                    nc.vector.scalar_tensor_tensor(out=ga[:, k % 2], in0=th[:, k % 2], scalar=1.0, in1=psG[k % 2],
                                                   op0=ALU.add, op1=ALU.mult).then_inc(s["f_a"], 1)

                def silu2(dst, t, z, sem):
                    nc.vector.scalar_tensor_tensor(out=dst, in0=t, scalar=1.0, in1=z, op0=ALU.add,
                                                   op1=ALU.mult).then_inc(s[sem], 1)

                def a_b(arg):
                    dve.wait_ge(s["a_eb"], arg[0] + 1)
                    silu2(at_base[:], at_bt[:], at_bz[:], "a_b")

                def a_qk(arg):
                    dve.wait_ge(s["a_b"], arg[0] + 1)
                    for dst, gamma, beta in ((at_q, qvec[:, 0:1], qvec[:, 1:2]), (at_k, v(V_GAMMA + 1), v(V_BETA + 1))):
                        ins = nc.vector.tensor_scalar(dst[:], at_base[:], gamma, beta, ALU.mult, ALU.add)
                    ins.then_inc(s["a_qk"], 1)

                def a_u(arg):
                    dve.wait_ge(s["a_eu"], arg[0] + 1)
                    silu2(at_u[:], at_ut, at_uz, "a_u")

                def a_v(arg):
                    dve.wait_ge(s["a_ev"], arg[0] + 1)
                    silu2(at_v[:], at_v[:], two(chainps), "a_v")

                def a_ua(arg):
                    dve.wait_ge(s["a_av"], arg[0] + 1)
                    dve.wait_ge(s["a_u"], arg[0] + 1)
                    nc.vector.scalar_tensor_tensor(out=at_u[:], in0=at_u[:], scalar=0.5, in1=two(chainps),
                                                   op0=ALU.mult, op1=ALU.mult).then_inc(s["a_ua"], 1)

                def a_x(arg):
                    a, b = arg
                    dve.wait_ge(s["a_tr"], a + 1)
                    name = f"x2_{b}"
                    nc.vector.tensor_tensor(xs[name][:], xs[name][:], two(chainps[:, T:2 * T]), ALU.add).then_inc(s["a_x"], 1)
                    dve.wait_ge(s["a_x"], a + 1)

                run_schedule({"setup": setup, "select": select, "m_stats": m_stats, "m_norm": m_norm, "m_lo": m_lo, "m_conv0": conv_tap(0),
                              "m_conv1": conv_tap(1), "m_conv2": conv_tap(2), "m_conv3": conv_tap(3), "m_g": m_g,
                              "m_h": m_h, "m_r": rest, "m_sel": m_sel, "m_c": m_c,
                              "m_l": m_l, "m_delta": m_delta, "dbx": dbx, "scan": scan, "mulC": mulC, "m_skip": m_skip,
                              "m_res": m_res, "n_stats": n_stats, "n_norm": n_norm, "n_lo": n_lo, "r_max": r_max,
                              "r_prob": r_prob, "r_top": r_top, "r_index": r_index, "r_weight": r_weight, "glu": glu,
                              "a_b": a_b, "a_qk": a_qk, "a_u": a_u, "a_v": a_v, "a_ua": a_ua,
                              "a_x": a_x}, schedule)

            @block.tensor
            def _(pe):
                reader = {"chain": None, "mamba": None}

                def free(bank):
                    if reader[bank]:
                        sem, value = reader[bank]
                        pe.wait_ge(s[sem], value)

                def transposes(bank, src):
                    for c in range(NC):
                        ins = nc.tensor.transpose(bank[:, c * P:(c + 1) * P], src[:, c * P:(c + 1) * P], ident[:])
                    return ins

                def three(bank, w, xv, start=True):
                    nc.tensor.matmul(bank, w[0], xv[0], start=start, stop=False)
                    nc.tensor.matmul(bank, w[0], xv[1], start=False, stop=False)
                    return nc.tensor.matmul(bank, w[1], xv[0], start=False, stop=True)

                def m_turn(arg):
                    p, b = arg
                    if first:
                        pe.wait_ge(s["w_const"], 1)
                    free("mamba")
                    pe.wait_ge(s["m_xm"], p + 1)
                    transposes(mambaps, m_xn[:].rearrange("p c h -> p (c h)")).then_inc(s["m_xt"], 1)
                    reader["mamba"] = ("m_lo", p + 1)

                def project(p, first_tile, sem):
                    free("mamba")
                    for it in range(IT):
                        cols = slice((first_tile + it) * P, (first_tile + it + 1) * P)
                        ins = three(two(mambaps)[:, it], (inw_hi[:, cols], inw_lo[:, cols]), (m_xhi[:], m_xlo[:]))
                    ins.then_inc(s[sem], 1)

                def m_ph(arg):
                    if first:
                        pe.wait_ge(s["w_inlo"], 1)
                    project(arg[0], 0, "m_ph")
                    reader["mamba"] = ("m_eh", arg[0] + 1)

                def m_pg(arg):
                    project(arg[0], IT, "m_pg")
                    reader["mamba"] = ("m_eg", arg[0] + 1)

                def m_xp(arg):
                    p, b = arg
                    if first:
                        pe.wait_ge(s["d_xpw"], 16)
                    free("mamba")
                    pe.wait_ge(s["m_h"], p + 1)
                    for it in range(IT):
                        ins = nc.tensor.matmul(mambaps[0:XP, 0:T], xpw[:, it, :], h[:, b, it], start=it == 0,
                                               stop=it == IT - 1)
                    ins.then_inc(s["m_xp"], 1)
                    reader["mamba"] = ("m_r", p + 1)

                def m_dt(arg):
                    p, b = arg
                    if first:
                        pe.wait_ge(s["d_dtw"], 16)
                    free("mamba")
                    for it in range(IT):
                        ins = nc.tensor.matmul(two(mambaps)[:, it], dtw[:, it * P:(it + 1) * P], ts[:], start=True, stop=True)
                    ins.then_inc(s["m_dt"], 1)
                    reader["mamba"] = ("m_z", p + 1)

                def rows(arg):
                    u, b, n, need = arg
                    r = u * (NS + 1) + n + 1
                    if first and r == 0:
                        pe.wait_ge(s["w_sel"], 1)
                    if need and n < 0:
                        pe.wait_ge(s["m_sel"], need)
                    used_b = u * NS + max(n, 0)
                    used_c = u * NS + (max(n - 1, 0) if n >= 0 else -1)
                    if used_b:
                        pe.wait_ge(s["m_dbx"], used_b)
                    if used_c > 0:
                        pe.wait_ge(s["m_p"], used_c)
                    if n >= 0:
                        ins = nc.tensor.matmul(rowps[r % 2][:, 1], sel[:, NS + n, :], bc_s[:, b], start=True, stop=True)
                    if n + 1 < NS:
                        ins = nc.tensor.matmul(rowps[r % 2][:, 0], sel[:, n + 1, :], bc_s[:, b], start=True, stop=True)
                    ins.then_inc(s["m_bc"], 1)

                def m_out(arg):
                    u, b = arg
                    if first:
                        pe.wait_ge(s["d_outw"], 16)
                    free("mamba")
                    pe.wait_ge(s["m_yg"], u + 1)
                    for it in range(IT):
                        ins = nc.tensor.matmul(mambaps[:, 0:T], outw[:, it, :], yacc[:, b, it], start=it == 0,
                                               stop=it == IT - 1)
                    ins.then_inc(s["m_out"], 1)

                def m_back(arg):
                    u, _ = arg
                    pe.wait_ge(s["m_yT"], u + 1)
                    transposes(mambaps[:, T:2 * T], yT).then_inc(s["m_ot"], 1)
                    reader["mamba"] = ("m_x1", u + 1)

                def n_turn(arg):
                    l = arg[0]
                    free("chain")
                    pe.wait_ge(s["n_xm"], l + 1)
                    transposes(chainps, n_xn[:].rearrange("p c h -> p (c h)")).then_inc(s["n_xt"], 1)
                    reader["chain"] = ("n_lo", l + 1)

                def r_logits(arg):
                    r, w = arg
                    if first:
                        pe.wait_ge(s["w_lo"], 3)
                    free("chain")
                    for c in range(NC):
                        cols = slice(c * P, (c + 1) * P)
                        ins = three(chainps[:, T + c * NE:T + (c + 1) * NE], (xhi[w][:, cols], xlo[w][:, cols]),
                                    (rw_hi[:], rw_lo[:]))
                    ins.then_inc(s["r_lg"], 1)
                    reader["chain"] = ("r_sub", r + 1)

                def products(bank, w, q, j, buf):
                    for k in range(2):
                        cols = slice((2 * j + k) * P, (2 * j + k + 1) * P)
                        ins = three(bank[:, k], (w[0][:, cols], w[1][:, cols]), (xhi[buf][:], xlo[buf][:]))
                    return ins

                def gate(arg):
                    q, j, buf, norms = arg
                    k = q * NP + j
                    if k >= 2:
                        pe.wait_ge(s["f_a"], k - 1)
                    if first and k == 0:
                        pe.wait_ge(s["w_lo"], 3)
                    if j == 0 and norms:
                        pe.wait_ge(s["n_lo"], norms)
                    products(psG[k % 2], (gate_hi, gate_lo), q, j, buf).then_inc(s["f_G"], 1)

                def up(arg):
                    q, j, buf, norms = arg
                    k = q * NP + j
                    if k:
                        pe.wait_ge(s["f_uc"], k)
                    elif first:
                        pe.wait_ge(s["w_lo"], 4)
                    products(psU, (up_hi, up_lo), q, j, buf).then_inc(s["f_U"], 1)

                def lower(arg):
                    q, e, *_ = arg
                    k = q * NE + e
                    if first and k == 0:
                        pe.wait_ge(s["d_down"], 16 * NB)
                    pe.wait_ge(s["f_in"], q * NP + last_pair(e) + 1)
                    if k:
                        pe.wait_ge(s["f_w"], k)
                    for c in range(NC):
                        for n in range(NB):
                            rows = min(P, FI - n * P)
                            pair, half_pair = divmod(NB * e + n, 2)
                            act_in = inner[0:rows, (q * NP + pair) % RING, half_pair, c * P:(c + 1) * P]
                            ins = nc.tensor.matmul(psO[:, c * H:(c + 1) * H], act_in, down[0:rows, e, n, :],
                                                   start=n == 0, stop=n == NB - 1)
                    ins.then_inc(s["f_dn"], 1)

                xa = (xhi["A"], xlo["A"])

                def a_pb(arg):
                    free("chain")
                    three(chainps[:, 0:T], (uv_hi[:, 4 * P:5 * P], uv_lo[:, 4 * P:5 * P]),
                          (xa[0][:], xa[1][:])).then_inc(s["a_pb"], 1)
                    reader["chain"] = ("a_eb", arg[0] + 1)

                def a_pu(arg):
                    free("chain")
                    for a in range(2):
                        cols = slice(a * P, (a + 1) * P)
                        ins = three(two(chainps)[:, a], (uv_hi[:, cols], uv_lo[:, cols]), (xa[0][:], xa[1][:]))
                    ins.then_inc(s["a_pu"], 1)
                    reader["chain"] = ("a_eu", arg[0] + 1)

                def a_pv(arg):
                    free("chain")
                    for c in range(NC):
                        cols = slice(c * P, (c + 1) * P)
                        bank = two(chainps)[:, c]
                        nc.tensor.matmul(bank, ones_row[:], vb_row[:], start=True, stop=False)
                        ins = three(bank, (xa[0][:, cols], xa[1][:, cols]),
                                    (uv_hi[:, 2 * P:4 * P], uv_lo[:, 2 * P:4 * P]), start=False)
                    ins.then_inc(s["a_pv"], 1)
                    reader["chain"] = ("a_v", arg[0] + 1)

                def a_sc(arg):
                    free("chain")
                    pe.wait_ge(s["a_qk"], arg[0] + 1)
                    for c in range(NC):
                        ins = nc.tensor.matmul(two(chainps)[:, c], at_k[:, c * P:(c + 1) * P], at_q[:], start=True, stop=True)
                    ins.then_inc(s["a_sc"], 1)
                    reader["chain"] = ("a_rl", arg[0] + 1)

                def a_av(arg):
                    free("chain")
                    pe.wait_ge(s["a_sq"], arg[0] + 1)
                    for a in range(2):
                        for c in range(NC):
                            ins = nc.tensor.matmul(two(chainps)[:, a], at_v[:, c, a * P:(a + 1) * P], at_s[:, c],
                                                   start=c == 0, stop=c == NC - 1)
                    ins.then_inc(s["a_av"], 1)
                    reader["chain"] = ("a_ua", arg[0] + 1)

                def a_wo(arg):
                    free("chain")
                    for a in range(2):
                        ins = nc.tensor.matmul(chainps[:, 0:T], wo[:, a, :], at_u[:, a], start=a == 0, stop=a == 1)
                    ins.then_inc(s["a_wo"], 1)

                def a_tr(arg):
                    pe.wait_ge(s["a_woT"], arg[0] + 1)
                    transposes(chainps[:, T:2 * T], at_oT).then_inc(s["a_tr"], 1)
                    reader["chain"] = ("a_x", arg[0] + 1)

                run_schedule({"m_turn": m_turn, "m_ph": m_ph, "m_pg": m_pg, "m_xp": m_xp, "m_dt": m_dt, "rows": rows,
                              "m_out": m_out, "m_back": m_back, "n_turn": n_turn, "r_logits": r_logits,
                              "gate": gate, "up": up, "down": lower, "a_pb": a_pb, "a_pu": a_pu,
                              "a_pv": a_pv, "a_sc": a_sc, "a_av": a_av, "a_wo": a_wo, "a_tr": a_tr}, schedule)

        numbers = [semaphore.num for semaphore in s.values()]
        sems = range(min(numbers), max(numbers) + 1)

        with ExitStack() as ctx2:
            block_of(ctx2, first_schedule(), [(0, 0, 0), (1, 1, 0), (2, 0, 1)], [], True)
        nc.all_engine_barrier(sems_to_clear=sems)
        with nc.Fori(1, sequences // 2) as g:
            with ExitStack() as ctx2:
                block_of(ctx2, middle_schedule(), [(2 * g + 1, 1, 0), ((2 * g + 2) % sequences, 0, 1)],
                         [(2, 2 * g - 2, "x3_0"), (4, 2 * g - 1, "x3_1")], False)
            nc.all_engine_barrier(sems_to_clear=sems)
        with ExitStack() as ctx2:
            block_of(ctx2, last_schedule(), [], [(2, sequences - 2, "x3_0"), (3, sequences - 1, "x3_1")], False)


def kernel(**inputs):
    import numpy as np
    import concourse.bacc as bacc
    from concourse.bass_utils import run_bass_kernel_spmd

    w = {k: np.asarray(a) for k, a in inputs.items()}
    a, b, f = "L0_attn_a_", "L0_attn_b_", "L0_ffn_"
    x = w[a + "x"]

    def cols(vector):
        return vector.reshape(-1, P).T

    conv_w = w[a + "conv_w"].reshape(KC, IT, P).transpose(2, 1, 0).reshape(P, IT * KC)
    a_log = w[a + "A_log"].reshape(IT, P, NS).transpose(1, 0, 2).reshape(P, IT * NS)
    uv_b = w[b + "b_uv"]
    vecs = np.concatenate([
        cols(w[a + "norm_scale"]), cols(w[a + "in_b"]), conv_w, cols(w[a + "conv_b"]), cols(w[a + "dt_b"]), a_log,
        cols(w[a + "D"]), cols(w[a + "out_b"]), cols(uv_b[0:2 * P]), cols(uv_b[4 * P:5 * P]),
        w[b + "gamma"].T, w[b + "beta"].T, cols(w[b + "b_out"])], axis=1)
    laid = {
        "x": x.reshape(-1, H),
        "vecs": vecs,
        "in_w": w[a + "in_w"],
        "xproj_w": w[a + "xproj_w"].reshape(IT, P, XP).transpose(1, 0, 2),
        "dt_w": w[a + "dt_w"],
        "out_w": w[a + "out_w"].reshape(IT, P, H).transpose(1, 0, 2),
        "gate_w": w[f + "w_gate"].transpose(1, 0, 2).reshape(H, NE * FI),
        "up_w": w[f + "w_up"].transpose(1, 0, 2).reshape(H, NE * FI),
        "down_w": w[f + "w_down"],
        "uv_w": w[b + "W_uv"],
        "v_b": uv_b[2 * P:4 * P].reshape(1, 2 * P),
        "wo_w": w[b + "W_out"].reshape(2, P, H).transpose(1, 0, 2),
        "router_w": w[f + "router_w"],
    }
    nc = bacc.Bacc("TRN2", target_bir_lowering=False, num_devices=1)
    arrays, args = {}, []
    for name, array in laid.items():
        arrays[name] = np.ascontiguousarray(array)
        args.append(nc.dram_tensor(name, array.shape, mybir.dt.from_np(array.dtype), kind="ExternalInput").ap())
    out = nc.dram_tensor("out", (x.shape[0] * x.shape[1], H), F32, kind="ExternalOutput").ap()
    build(nc, *args, out)
    result = run_bass_kernel_spmd(nc, [arrays], core_ids=[0])
    return result.results[0]["out"].reshape(x.shape)
```
